# Optimizing a Trainium2 kernel written in Bass

```python
import numpy as np
import jax
import jax.numpy as jnp

def _softmax(x, axis=-1):
    return jax.nn.softmax(x, axis=axis)

def _gelu(x):
    return jax.nn.gelu(x, approximate=True)

def _silu(x):
    return jax.nn.silu(x)

def _sigmoid(x):
    return jax.nn.sigmoid(x)

def _layernorm(x, axis=-1, eps=1e-05):
    m = jnp.mean(x, axis=axis, keepdims=True)
    v = jnp.var(x, axis=axis, keepdims=True)
    return (x - m) / jnp.sqrt(v + eps)

def _scatter_add(tgt, idx, src, axis=0):
    return tgt.at[idx].add(src)

def _segment_sum(src, seg, n):
    return jax.ops.segment_sum(src, seg, n)
kernel_name = 'mk_pixart_resid_d1_seqx_r4_b0005e'

def setup_inputs(seed: int=0):
    np.random.seed(seed)
    _w = jnp.asarray

    def _rec_inputs():
        import jax
        import jax.numpy as jnp
        _rk = jax.random.key(seed)
        x = -0.0002928 + 1 * jax.random.normal(jax.random.fold_in(_rk, 1), (16, 128, 512), jnp.float32)
        _lenS = 128 - jax.random.randint(jax.random.fold_in(_rk, 7), (16,), 0, max(1, 128 // 4) + 1, jnp.int32)
        _lenS2 = 128 - jax.random.randint(jax.random.fold_in(_rk, 8), (16,), 0, max(1, 128 // 4) + 1, jnp.int32)
        _ctx_2048P = jax.random.normal(jax.random.fold_in(_rk, 11), (16, 16, 512), jnp.float32)
        _ctx_2048c = jax.random.dirichlet(jax.random.fold_in(_rk, 511), 0.3 * jnp.ones((16,), jnp.float32), (16, 128))
        _ctx_2048t = jnp.einsum('bsk,bkd->bsd', _ctx_2048c, _ctx_2048P)
        _ctx_2048t = _ctx_2048t * jax.lax.rsqrt(jnp.mean(jnp.square(_ctx_2048t)) + 1e-12) * 0.953939
        ctx_2048 = -1.39393e-06 + 0.999914 * (_ctx_2048t + 0.3 * jax.random.normal(jax.random.fold_in(_rk, 611), (16, 128, 512), jnp.float32))
        itok_B_779_1933 = jax.random.randint(jax.random.fold_in(_rk, 12), (16,), 779, 1934, jnp.int32)
        return (x, ctx_2048, itok_B_779_1933)
    x, ctx_2048, itok_B_779_1933 = _rec_inputs()

    def _L0_xcond_setup():
        import jax, jax.numpy as jnp
        import numpy as np
        NUM_HEADS = 8
        HEAD_DIM = 64
        AVG_K_LENGTH = 20
        SCALE = 1.0 / (HEAD_DIM ** 0.5 * float(np.log(AVG_K_LENGTH)))
        key = jax.random.key(seed)
        k1, k2, k3, k4 = jax.random.split(key, 4)
        B, HD, LQ, LK = (4, NUM_HEADS * HEAD_DIM, 512, 512)
        q = jax.random.normal(k1, (B, HD, LQ), dtype=jnp.float32)
        k = jax.random.normal(k2, (B, HD, LK), dtype=jnp.float32)
        v = jax.random.normal(k3, (B, HD, LK), dtype=jnp.float32)
        k_length = jax.random.randint(k4, (B,), 128, LK + 1, dtype=jnp.int32)
        return {'q': q, 'k': k, 'v': v, 'k_length': k_length}
    _L0_xcond_all = _L0_xcond_setup()
    _L0_xcond_in = {k: v for k, v in _L0_xcond_all.items() if k in ()}
    del _L0_xcond_all

    def _L0_ffn_setup():
        import jax, jax.numpy as jnp
        import numpy as np
        NUM_ACT = 2
        key = jax.random.key(seed)
        k1, k2, k3, k4, k5 = jax.random.split(key, 5)
        B, S, D, I, E = (4, 128, 512, 1024, 8)
        x = jax.random.normal(k1, (B, S, D), dtype=jnp.float32)
        gate_w = jax.random.normal(k2, (E, D), dtype=jnp.float32) * 0.02
        w1 = jax.random.normal(k3, (E, I, D), dtype=jnp.float32) * 0.02
        w2 = jax.random.normal(k4, (E, D, I), dtype=jnp.float32) * 0.02
        w3 = jax.random.normal(k5, (E, I, D), dtype=jnp.float32) * 0.02
        return {'x': x, 'gate_w': gate_w, 'w1': w1, 'w2': w2, 'w3': w3}
    _L0_ffn_all = _L0_ffn_setup()
    _L0_ffn_in = {k: v for k, v in _L0_ffn_all.items() if k in ('gate_w', 'w1', 'w2', 'w3')}
    del _L0_ffn_all
    return {'x': x, 'ctx_2048': ctx_2048, 'itok_B_779_1933': itok_B_779_1933, 'L0_ffn_gate_w': _L0_ffn_in['gate_w'], 'L0_ffn_w1': _L0_ffn_in['w1'], 'L0_ffn_w2': _L0_ffn_in['w2'], 'L0_ffn_w3': _L0_ffn_in['w3']}

def reference(x, ctx_2048, itok_B_779_1933, L0_ffn_gate_w, L0_ffn_w1, L0_ffn_w2, L0_ffn_w3):
    import jax
    import jax.numpy as jnp

    def _L0_xcond_ref(q, k, v, k_length):
        import jax, jax.numpy as jnp
        import numpy as np
        NUM_HEADS = 8
        HEAD_DIM = 64
        AVG_K_LENGTH = 20
        SCALE = 1.0 / (HEAD_DIM ** 0.5 * float(np.log(AVG_K_LENGTH)))
        b, hd, lq = q.shape
        lk = k.shape[-1]
        d = hd // NUM_HEADS
        qh = q.reshape(b, NUM_HEADS, d, lq)
        kh = k.reshape(b, NUM_HEADS, d, lk)
        vh = v.reshape(b, NUM_HEADS, d, lk)
        s = SCALE * jnp.log(k_length.astype(jnp.float32))[:, None, None, None]
        attn = jnp.einsum('bhdq,bhdk->bhqk', qh, kh)
        attn = jax.nn.softmax(s * attn, axis=-1)
        out = jnp.einsum('bhqk,bhdk->bhdq', attn, vh)
        return out.reshape(b, hd, lq)

    def _L0_ffn_ref(x, gate_w, w1, w2, w3):
        import jax, jax.numpy as jnp
        import numpy as np
        NUM_ACT = 2
        B, S, D = x.shape
        xt = x.reshape(-1, D)
        scores = jnp.einsum('ti,ei->te', xt, gate_w)
        probs = jax.nn.softmax(scores, axis=-1)
        expert_weights, expert_indices = jax.lax.top_k(probs, NUM_ACT)
        expert_weights = expert_weights / expert_weights.sum(axis=-1, keepdims=True)
        x1 = jax.nn.silu(jnp.einsum('ti,eoi->teo', xt, w1))
        x3 = jnp.einsum('ti,eoi->teo', xt, w3)
        expert_outs_all = jnp.einsum('teo,eio->tei', x1 * x3, w2)
        sel = jnp.take_along_axis(expert_outs_all, expert_indices[:, :, None], axis=1)
        out = jnp.einsum('tai,ta->ti', sel, expert_weights)
        return out.reshape(B, S, D)
    x = x + _L0_xcond_ref(_layernorm(x, axis=-1), ctx_2048, ctx_2048, itok_B_779_1933)
    x = x + _L0_ffn_ref(_layernorm(x, axis=-1), L0_ffn_gate_w, L0_ffn_w1, L0_ffn_w2, L0_ffn_w3)
    return x

_drawn_inputs = setup_inputs


def setup_inputs(seed=0):
    import zlib

    import numpy as np

    out = dict(_drawn_inputs(seed))
    spreads = {}
    factors = {}
    for name, (base, spread) in spreads.items():
        noise = np.random.default_rng([zlib.crc32(name.encode()), seed]).standard_normal(out[name].shape)
        drawn = base * np.exp(spread * noise) if base else spread * noise
        out[name] = jnp.asarray(drawn.astype(out[name].dtype))
    for name, factor in factors.items():
        out[name] = (out[name] * factor).astype(out[name].dtype)
    return out
```

```python
from contextlib import ExitStack

import numpy as np

import concourse.bass as bass
from concourse import mybir

ALU = mybir.AluOpType
ACT = mybir.ActivationFunctionType
F32 = mybir.dt.float32
BF16 = mybir.dt.bfloat16
I32 = mybir.dt.int32
AX_X = mybir.AxisListType.X

P = 128
LOOP_FIRST, LOOP_LAST = 2, 6
ENGINE_STEPS = {"prep": 14, "z": 4, "route_a": 14, "route_b": 16}


class Batch:

    def __init__(self, pair, parity, low, high):
        self.pair, self.parity = pair, parity
        self.low, self.high = low, high

    @property
    def n(self):
        return self.pair * 2 + self.parity

    def plus(self, k):
        p = self.parity + k
        return Batch(self.pair + p // 2, p % 2, self.low + k, self.high + k)

    def within(self, first, last):
        inside = first <= self.low and self.high <= last
        assert inside or self.high < first or self.low > last
        return inside


class Steps:

    def __init__(self, wait, sem, index, each):
        self.wait, self.sem, self.index, self.each, self.done = wait, sem, index, each, 0

    def step(self, instruction):
        self.done += 1
        instruction.then_inc(self.sem, 1)
        self.wait(self.sem, self.index * self.each + self.done)

    def end(self):
        assert self.done == self.each, (self.done, self.each)


def build(nc, x, ctx_kv, lengths, wpack, gate_t, out):
    B, HD, L = x.shape
    LK = ctx_kv.shape[2]
    H = 8
    DH = HD // H
    E, _, WLEN = wpack.shape
    D = L
    I = WLEN // (3 * D // P)
    KD, KI = D // P, I // P
    assert WLEN == KD * I * 2 + KI * D and HD == P and L == LK == 512
    SCALE = 1.0 / (64 ** 0.5 * float(np.log(20)))
    EPS = 1e-5
    BIG = 3.0e38
    TOK = B * P
    REG = TOK + P
    T = (2 * TOK + E * (P - 1)) // P
    CH = 1024
    NCH = WLEN // CH
    KROWS, MROW = 6 * DH, 6 * DH

    pd = nc.dram_tensor("parts_dram", [B, P, 6, L], BF16, kind="Internal").ap()
    zs = nc.dram_tensor("slots_dram", [E * REG, D], F32, kind="Internal").ap()
    ys = nc.dram_tensor("expert_out_dram", [T * P, D], F32, kind="Internal").ap()
    sums_dram = nc.dram_tensor("sums_dram", [B, H, L], F32, kind="Internal").ap()
    recips_dram = nc.dram_tensor("recips_dram", [B, H, L], F32, kind="Internal").ap()
    maxima_dram = nc.dram_tensor("maxima_dram", [B, 2, H * L], BF16, kind="Internal").ap()
    wp = wpack

    with ExitStack() as cx:
        def sb(name, shape, dt):
            return cx.enter_context(nc.sbuf_tensor(name, shape, dt))

        def pb(name, shape, dt=F32):
            return cx.enter_context(nc.psum_tensor(name, shape, dt))

        def sem(name):
            return cx.enter_context(nc.semaphore(name))

        xres = sb("xres", [P, B, L], F32)
        W = sb("W", [P, 2 * 2 * WLEN], BF16)
        stage = sb("stage", [P, 2, CH], F32)
        ident = sb("ident", [P, P], F32)
        em8 = sb("em8", [P, E], F32)
        first_mx = sb("first_mx", [P, B], F32)
        second_mx = sb("second_mx", [P, B], F32)
        rank = sb("rank", [P, 2, B], F32)
        gdiff = sb("gdiff", [P, B], F32)

        half = 2 * WLEN
        probs = W[:, half:half + 16384].bitcast(F32).rearrange("p (b j k q) -> p b j k q", b=2, j=4, k=2)
        ks = W[:, half + 16384:half + 24576].rearrange("p (b h k) -> p b h k", b=2, h=H)
        U = sb("U", [P, 11264], F32)
        qs = U[:, 0:4096].bitcast(BF16).rearrange("p (b h q) -> p b h q", b=2, h=H)
        parts = U[:, 4096:7168].bitcast(BF16).rearrange("p (b c q) -> p b c q", b=2, c=6)
        vt = U[:, 7168:9216].rearrange("p (b k h c) -> p b k h c", b=2, k=4, h=H)
        cin = U[:, 9216:10240].rearrange("p (b k) -> p b k", b=2)
        og = U[:, 10240:11264].rearrange("p (g q) -> p g q", g=2)
        cv = sb("cv", [P, LK], F32)
        norm = sb("norm", [P, L], F32)
        rest = sb("rest", [P, L], F32)
        us = sb("us", [P, L], F32)
        tb = sb("tb", [P, L], F32)
        x1 = sb("x1", [P, L], F32)
        z = sb("z", [P, 2, D], F32)
        zt = sb("zt", [P, KD, P], F32)
        selu = sb("selu", [P, 2, P], F32)
        selb = sb("selb", [8, P], F32)
        r8 = sb("r8", [8, L], F32)
        den = sb("den", [P, 32], F32)
        rden = sb("rden", [P, 32], F32)
        nm = sb("nm", [P, 2, P], F32)
        mrow = sb("mrow", [32, 2, P], BF16)
        len_i = sb("len_i", [P, B], I32)
        len_f = sb("len_f", [P, B], F32)
        len_ln = sb("len_ln", [P, B], F32)
        sb_col = sb("sb_col", [P, B], F32)
        st1 = sb("st1", [P, 6], F32)
        mv1 = sb("mv1", [P, 2, 2], F32)
        st2 = sb("st2", [P, 6], F32)
        mv2 = sb("mv2", [P, 2], F32)
        mhalf = sb("mhalf", [P, 1], F32)
        zero = sb("zero", [P, 1], F32)
        psc = sb("psc", [P, 4], F32)
        zsc = sb("zsc", [P, 4], F32)
        gw = sb("gw", [P, KD, E], F32)
        gs = sb("gs", [P, 2, E], F32)
        masks = sb("masks", [P, 2, 2, E], F32)
        rt = sb("rt", [P, 6, 2, E], F32)
        rc = sb("rc", [P, 8, 2], F32)
        maskb = sb("maskb", [P, 2, E], BF16)
        ltri = sb("ltri", [P, P], BF16)
        onesb = sb("onesb", [P, P], BF16)
        cnt = sb("cnt", [P, E], F32)
        idx = sb("idx", [P, 2, 2], I32)
        tl_i = sb("tl_i", [P, E], I32)
        tl = sb("tl", [P, 4, E], F32)
        tio_i = sb("tio_i", [P, T], I32)
        tio = sb("tio", [P, T], F32)
        t3 = U[:, 7168:7168 + T * E].rearrange("p (t e) -> p t e", e=E)
        tt = U[:, 8192:8192 + 5 * T].rearrange("p (n t) -> p n t", n=5)
        tab = sb("tab", [P, 3, T], I32)
        etab = sb("etab", [P, 2, E], I32)
        fidx = sb("fidx", [P, 2, B], I32)
        f3 = t3[:, 0:B, :]
        ff = sb("ff", [P, B], F32)
        gexp = sb("gexp", [P, B], F32)
        gsum = sb("gsum", [P, B], F32)
        gate = sb("gate", [P, 2, B], F32)

        xrow = U[:, 0:1024].rearrange("p (b d) -> p b d", b=2)
        xT = U[:, 1024:2048].bitcast(BF16).rearrange("p (b s k t) -> p b s k t", b=2, s=2, k=KD)
        act_g = U[:, 2048:3072]
        hbuf = U[:, 3072:4096]
        hT = U[:, 4096:6144].bitcast(BF16).rearrange("p (b s k t) -> p b s k t", b=2, s=2, k=KI)
        yb = U[:, 6144:7168].rearrange("p (b d) -> p b d", b=2)
        gb = U[:, 7168:11264].rearrange("p (b a d) -> p b a d", b=4, a=2)

        sc = [pb(f"scores{i}", [P, 512]) for i in range(2)]
        p1 = [pb(f"rows{i}", [P, 1024]) for i in range(2)]
        ob = pb("heads_out", [P, 512])
        misc = pb("misc", [P, 512])
        up = [[p1[0][:, 0:512], p1[1][:, 0:512]], [p1[0][:, 512:1024], p1[1][:, 512:1024]]]
        hTp = [sc[0], sc[1]]

        names = """setup consts rows_set gate_in len_in ln_ready sb_ready chain table_chain prep_steps z_steps
            route_a_steps route_b_steps pd_out sums_out rec_out m_out den_in rec_in m_in cv_in p1_ready p1_used scores_ready
            exp_done pv_done og_ready vt_ps vt_ready u_ready us_ready r_ready t_ready x1_ready x1_kept zt_ps zt_ready
            gate_ready gate_copied mask_ready rank_ready rank_used idx_ready slots_out rec_ready st1_steps
            st2_steps st1_ready st2_ready prep_done z_ready mt_ready m_steps m_ready chunk_steps w_ready
            tab_ready zero_out tiles_done xt_ps xt_hi xt_lo up_ready silu_done h_ready ht_ps ht_hi ht_lo
            yb_ready pool_held dve_held sp_held gexp_ready gate_w_ready comb_steps comb_done out_done attn_done routed""".split()
        S = {n: sem(n) for n in names}
        loads = [sem(f"loads{i}") for i in range(2)]
        st_in = [[sem(f"stack{i}{j}") for j in range(2)] for i in range(2)]
        w_in = [sem(f"w_in{i}") for i in range(2)]
        xrow_in = [sem(f"xrow_in{i}") for i in range(2)]
        y_out = [sem(f"y_out{i}") for i in range(2)]
        g_in = [sem(f"g_in{i}") for i in range(4)]

        def slots(engine, body):
            for b in range(-3, 2 * LOOP_FIRST):
                body(Batch(b // 2, b % 2, b, b))
            with engine.Fori(LOOP_FIRST, LOOP_LAST) as i:
                for par in range(2):
                    body(Batch(i, par, 2 * LOOP_FIRST + par, 2 * LOOP_LAST - 2 + par))
            for b in range(2 * LOOP_LAST, B + 2):
                body(Batch(b // 2, b % 2, b, b))

        def at(tensor, i):
            return bass.ds(i, 1)

        N_CONST = 12
        block = cx.enter_context(nc.Block())

        @block.sync
        def _(sp):
            sp.dma_start(len_i[:, :], lengths.partition_broadcast(P)).then_inc(S["len_in"], 16)
            sp.dma_start(gw[:, :, :], gate_t.rearrange("(k p) e -> p k e", p=P)).then_inc(S["gate_in"], 16)
            sp.wait_ge(S["consts"], N_CONST)

            def reload(b, half_h):
                heads = slice(4 * half_h, 4 * half_h + 4)
                src = pd[bass.ds(b.n, 1)].rearrange("o p c q -> (o p) c q") \
                    .rearrange("(h d) c q -> c d h q", h=H)
                row = 0
                for n in (3, 2, 1):
                    sp_q = src[0:n, :, heads, :]
                    for c in range(n):
                        r = row + DH * c
                        sp.dma_start(qs[r:r + DH, b.parity, heads, :], src[c, :, heads, :]) \
                            .then_inc(st_in[b.parity][half_h], 16)
                        sp.dma_start(ks[r:r + DH, b.parity, heads, :], src[3 + 3 - n, :, heads, :]) \
                            .then_inc(st_in[b.parity][half_h], 16)
                    row += DH * n

            def slot(b):
                nb = b.plus(1)
                if nb.within(0, B - 1):
                    if b.within(1, B):
                        sp.wait_ge(S["scores_ready"], b.n * 32)
                    reload(nb, 1)
                lb = b.plus(3)
                if lb.within(0, B - 1):
                    if b.within(-1, B):
                        sp.wait_ge(S["prep_done"], b.n + 2)
                    sp.dma_start(xres[:, at(xres, lb.n), :], x[bass.ds(lb.n, 1)].rearrange("o p q -> p o q")) \
                        .then_inc(loads[lb.parity], 16)
                    sp.dma_start(cin[:, lb.parity, :], ctx_kv[bass.ds(lb.n, 1)].rearrange("o p q -> p (o q)")) \
                        .then_inc(loads[lb.parity], 16)
                pv, pbt = b.plus(-1), b.plus(2)
                behind, ahead2 = pv.within(0, B - 1), pbt.within(0, B - 1)
                if behind:
                    sp.wait_ge(S["og_ready"], b.n * 2)
                    for g in range(2):
                        sp.dma_start(sums_dram[bass.ds(pv.n, 1), 4 * g:4 * g + 4].rearrange("o h q -> (o h) q"),
                                     og[16:113:32, g, :]).then_inc(S["sums_out"], 16)
                    sp.wait_ge(S["sums_out"], b.n * 32)
                    sp.dma_start(den[:, :], sums_dram[bass.ds(pv.n, 1)].rearrange("o h (p f) -> (o h p) f", f=32)) \
                        .then_inc(S["den_in"], 16)
                if ahead2:
                    sp.wait_ge(S["prep_done"], b.n + 3)
                    sp.dma_start(pd[bass.ds(pbt.n, 1)].rearrange("o p c q -> p (o c) q"),
                                 parts[:, pbt.parity]).then_inc(S["pd_out"], 16)
                if behind:
                    sp.wait_ge(S["rec_ready"], b.n)
                    sp.dma_start(recips_dram[bass.ds(pv.n, 1)].rearrange("o h (p f) -> (o h p) f", f=32),
                                 rden[:, :]).then_inc(S["rec_out"], 16)
                    sp.wait_ge(S["rec_out"], b.n * 16)
                    sp.nop().then_inc(S["sp_held"], 1)
                    if b.within(2, B):
                        sp.wait_ge(S["r_ready"], b.n - 1)
                    sp.dma_start(r8[:, :], recips_dram[bass.ds(pv.n, 1)].rearrange("o h q -> (o h) q")) \
                        .then_inc(S["rec_in"], 16)
                if ahead2:
                    sp.wait_ge(S["pd_out"], b.n * 16 + 48)
                    sp.nop().then_inc(S["sp_held"], 1)
                    if b.within(0, B - 1):
                        sp.wait_ge(S["scores_ready"], b.n * 32 + 16)
                    reload(pbt, 0)
                if nb.within(0, B - 1):
                    sp.wait_ge(S["m_ready"], b.n + 2)
                    sp.dma_start(maxima_dram[bass.ds(nb.n, 1)].rearrange("o s (c q) -> c (o s) q", q=P),
                                 mrow[:, :, :]).then_inc(S["m_out"], 16)
                    sp.wait_ge(S["m_out"], b.n * 16 + 32)
                    sp.dma_start(qs[MROW:MROW + 2, nb.parity],
                                 maxima_dram[bass.ds(nb.n, 1)].rearrange("o s (h q) -> (o s) h q", h=H)) \
                        .then_inc(S["m_in"], 16)
                if pbt.within(0, B - 1):
                    if nb.within(0, B - 1):
                        sp.wait_ge(S["vt_ps"], b.n + 2)
                    sp.dma_start(cv[:, :], ctx_kv[bass.ds(pbt.n, 1)].rearrange("o p q -> p (o q)")) \
                        .then_inc(S["cv_in"], 16)

            slots(sp, slot)

            sp.wait_ge(S["tab_ready"], 1)
            for e in range(E):
                r = sp.value_load(etab[0:1, 0, e:e + 1], min_val=0, max_val=E * REG - P)
                sp.dma_start(zs[bass.ds(r, P), :], cv[:, :]).then_inc(S["zero_out"], 16)
            sp.wait_ge(S["zero_out"], 16 * E)
            sp.wait_ge(S["slots_out"], 64 * (B // 2))

            def load_tile(t, par):
                r = sp.value_load(tab[0:1, 0, bass.ds(t, 1)], min_val=0, max_val=E * REG - P)
                sp.dma_start(xrow[:, par, :], zs[bass.ds(r, P), :]).then_inc(xrow_in[par], 16)

            def store_tile(t, par):
                sp.wait_ge(S["yb_ready"], t + 1)
                sp.dma_start(ys[bass.ds(t * P, P), :], yb[:, par, :]).then_inc(y_out[par], 16)

            load_tile(0, 0)
            load_tile(1, 1)
            with sp.Fori(0, (T - 3) // 2) as i:
                for par in range(2):
                    sp.wait_ge(S["xt_ps"], i * 2 + par + 1)
                    load_tile(i * 2 + par + 2, par)
                    store_tile(i * 2 + par, par)
            sp.wait_ge(S["xt_ps"], T - 2)
            load_tile(T - 1, 0)
            store_tile(T - 3, 0)
            store_tile(T - 2, 1)
            store_tile(T - 1, 0)

            with sp.Fori(0, B) as b:
                sp.wait_ge(S["comb_done"], b + 1)
                sp.dma_start(out[bass.ds(b, 1)].rearrange("o p d -> p o d"), xres[:, bass.ds(b, 1), :]) \
                    .then_inc(S["out_done"], 16)
            sp.wait_ge(S["out_done"], 16 * B)

        @block.gpsimd
        def _(pool):
            g = nc.gpsimd

            def hold(semaphore, value):
                pool.wait_ge(semaphore, value)
                g.nop().then_inc(S["pool_held"], 1)

            k = S["setup"]
            g.memset(ident[:, :], 0.0).then_inc(k, 1)
            g.memset(selu[:, :, :], 0.0).then_inc(k, 1)
            g.memset(selb[:, :], 0.0).then_inc(k, 1)
            g.memset(ltri[:, :], 1.0).then_inc(k, 1)
            g.memset(vt, 0.0).then_inc(k, 1)
            hold(k, 5)
            c = S["consts"]
            g.affine_select(out=ident[:, :], in_=ident[:, :], compare_op=ALU.not_equal, fill=1.0, base=0,
                            pattern=[[-1, P]], channel_multiplier=1).then_inc(c, 1)
            for gr in range(2):
                v = selu[:, gr, :].rearrange("p (h d) -> p h d", h=H)
                g.affine_select(out=v, in_=v, compare_op=ALU.not_equal, fill=1.0, base=128 * gr,
                                pattern=[[-32, H], [-1, DH]], channel_multiplier=1).then_inc(c, 1)
            v = selb[:, :].rearrange("p (h d) -> p h d", h=H)
            g.affine_select(out=v, in_=v, compare_op=ALU.not_equal, fill=1.0, base=0,
                            pattern=[[-1, H], [0, DH]], channel_multiplier=1).then_inc(c, 1)
            g.affine_select(out=ltri[:, :], in_=ltri[:, :], compare_op=ALU.is_gt, fill=0.0, base=0,
                            pattern=[[1, P]], channel_multiplier=-1).then_inc(c, 1)
            g.memset(onesb[:, :], 1.0).then_inc(c, 1)
            g.memset(vt[:, :, :, :, DH:DH + 1], 1.0).then_inc(c, 1)
            g.memset(nm[:, :, :], 0.0).then_inc(c, 1)
            g.memset(cnt[:, :], 0.0).then_inc(c, 1)
            g.memset(mhalf[:, :], -0.5).then_inc(c, 1)
            g.memset(zero[:, :], 0.0).then_inc(c, 1)
            for e in range(E):
                ins = g.memset(em8[:, e:e + 1], float(e - E))
            ins.then_inc(c, 1)
            g.iota(tio_i[:, :], pattern=[[1, T]], base=0, channel_multiplier=0).then_inc(S["table_chain"], 1)
            hold(c, N_CONST)

            def high_low(steps, dst_hi, dst_lo, src, tmp=None, moving=False):
                if moving:
                    steps.step(g.tensor_tensor(dst_hi, src, zero[:, :].to_broadcast(src.shape), ALU.add))
                else:
                    steps.step(g.tensor_scalar(dst_hi, src, 1.0, 0.0, ALU.mult, ALU.add))
                steps.step(g.tensor_tensor(tmp if tmp is not None else dst_lo, src, dst_hi, ALU.subtract))

            def split_chunk(dst_half, col, n, n_pair, par, moving=False):
                steps = Steps(hold, S["chunk_steps"], n, 2)
                hold(w_in[par], n_pair * 16 + 16)
                base = dst_half * half
                high_low(steps, W[:, bass.ds(col + base, CH)], W[:, bass.ds(col + (base + WLEN), CH)],
                         stage[:, par, :], moving=moving)
                steps.end()

            def slot(b):
                pbt = b.plus(2)
                if pbt.within(0, B - 1):
                    st = Steps(hold, S["prep_steps"], pbt.n, ENGINE_STEPS["prep"])
                    hold(S["st1_ready"], b.n + 3)
                    if pbt.within(0, 0):
                        hold(S["sb_ready"], 1)
                    if pbt.within(2, B - 1):
                        hold(S["pd_out"], b.n * 16 + 16)
                    mean, var = mv1[:, pbt.parity, 0:1], mv1[:, pbt.parity, 1:2]
                    st.step(g.tensor_scalar(psc[:, 0:1], var, EPS, 1.0, ALU.add, ALU.mult))
                    st.step(g.tensor_tensor(psc[:, 1:2], psc[:, 0:1], mhalf[:, :], ALU.pow))
                    st.step(g.tensor_tensor(psc[:, 2:3], psc[:, 1:2], sb_col[:, bass.ds(pbt.n, 1)], ALU.mult))
                    st.step(g.tensor_scalar(psc[:, 3:4], mean, -1.0, 0.0, ALU.mult, ALU.add))
                    st.step(g.tensor_tensor(norm[:, :], xres[:, at(xres, pbt.n), :].rearrange("p o q -> p (o q)"),
                                            psc[:, 3:4].to_broadcast([P, L]), ALU.add))
                    st.step(g.tensor_scalar(norm[:, :], norm[:, :], psc[:, 2:3], 0.0, ALU.mult, ALU.add))
                    pt = parts[:, pbt.parity]
                    for c0, src in ((0, norm[:, :]), (3, cin[:, pbt.parity, :])):
                        high_low(st, pt[:, c0, :], None, src, rest[:, :])
                        high_low(st, pt[:, c0 + 1, :], pt[:, c0 + 2, :], rest[:, :])
                    st.end()
                    g.nop().then_inc(S["prep_done"], 1)
                if b.parity == 1 and b.within(3, B + 1):
                    pair = b.pair - 1
                    hold(S["idx_ready"], pair + 1)
                    for s in range(2):
                        for a in range(2):
                            pool.indirect_dma_start(
                                out=zs[:, :], out_offset=bass.IndirectOffsetOnAxis(ap=idx[:, s, a:a + 1], axis=0),
                                in_=z[:, s, :], in_offset=None).then_inc(S["slots_out"], 16)
                pv = b.plus(-1)
                if pv.within(0, B - 1):
                    hold(S["t_ready"], b.n)
                    if pv.within(1, B - 1):
                        hold(S["x1_kept"], b.n - 1)
                    xr = xres[:, at(xres, pv.n), :].rearrange("p o q -> p (o q)")
                    g.tensor_tensor(x1[:, :], xr, tb[:, :], ALU.add).then_inc(S["x1_ready"], 1)
                    hold(S["st2_ready"], b.n)
                    st = Steps(hold, S["z_steps"], pv.n, ENGINE_STEPS["z"])
                    if pv.within(2, B - 1):
                        hold(S["zt_ps"], b.n - 2)
                        hold(S["slots_out"], (pv.pair) * 64)
                    st.step(g.tensor_scalar(zsc[:, 0:1], mv2[:, 1:2], EPS, 1.0, ALU.add, ALU.mult))
                    st.step(g.tensor_tensor(zsc[:, 1:2], zsc[:, 0:1], mhalf[:, :], ALU.pow))
                    st.step(g.tensor_scalar(zsc[:, 2:3], mv2[:, 0:1], -1.0, 0.0, ALU.mult, ALU.add))
                    st.step(g.tensor_scalar(z[:, pv.parity, :], x1[:, :], zsc[:, 2:3], zsc[:, 1:2], ALU.add, ALU.mult))
                    st.end()
                    g.nop().then_inc(S["z_ready"], 1)
                if b.within(1, 1):
                    for n in range(2):
                        pool.dma_start(stage[:, n, :], wp[0, :, n * CH:(n + 1) * CH]).then_inc(w_in[n], 16)
                if b.within(2, 1 + NCH):
                    n = b.n - 2
                    split_chunk(0, n * CH, n, b.pair - 1, b.parity, moving=True)
                    if b.within(2, NCH - 1):
                        pool.dma_start(stage[:, b.parity, :], wp[0, :, bass.ds((n + 2) * CH, CH)]) \
                            .then_inc(w_in[b.parity], 16)
                    if b.within(1 + NCH, 1 + NCH):
                        g.nop().then_inc(S["w_ready"], 1)

            slots(pool, slot)

            def expert(e, e_par, n0):
                for ch in range(2):
                    pool.dma_start(stage[:, ch, :], wp[bass.ds(e, 1), :, ch * CH:(ch + 1) * CH].rearrange(
                        "o p c -> p (o c)")).then_inc(w_in[ch], 16)
                for ch in range(NCH):
                    split_chunk(e_par, ch * CH, n0 + ch, (n0 + ch - ch % 2) // 2 if isinstance(n0, int)
                                else e * (NCH // 2) + ch // 2, ch % 2)
                    if ch + 2 < NCH:
                        pool.dma_start(stage[:, ch % 2, :], wp[bass.ds(e, 1), :, (ch + 2) * CH:(ch + 3) * CH]
                                       .rearrange("o p c -> p (o c)")).then_inc(w_in[ch % 2], 16)
                g.nop().then_inc(S["w_ready"], 1)

            hold(S["attn_done"], 1)
            expert(1, 1, NCH)
            hold(S["tab_ready"], 1)
            with pool.Fori(1, E // 2) as i:
                for par in range(2):
                    e = i * 2 + par
                    last = pool.value_load(etab[0:1, 1, bass.ds(e - 2, 1)], min_val=1, max_val=T + 1)
                    hold(S["tiles_done"], last)
                    expert(e, par, e * NCH)

            hold(y_out[0], 16 * ((T + 1) // 2))
            hold(y_out[1], 16 * (T // 2))

            def gather(b, r):
                for a in range(2):
                    pool.indirect_dma_start(
                        out=gb[:, r, a, :], out_offset=None, in_=ys[:, :],
                        in_offset=bass.IndirectOffsetOnAxis(ap=fidx[:, a, b:b + 1], axis=0)) \
                        .then_inc(g_in[r], 16)

            for b in range(B):
                if b >= 4:
                    hold(S["comb_done"], b - 3)
                gather(b, b % 4)

        @block.scalar
        def _(act):
            s = nc.scalar
            act.wait_ge(S["len_in"], 16)
            s.activation(len_f[:, :], len_i[:, :], ACT.Copy).then_inc(S["ln_ready"], 1)
            act.wait_ge(S["ln_ready"], 1)
            s.activation(len_ln[:, :], len_f[:, :], ACT.Ln).then_inc(S["ln_ready"], 1)

            def slot(b):
                nb, pv, pv2 = b.plus(1), b.plus(-1), b.plus(-2)
                full, behind = b.within(0, B - 1), pv.within(0, B - 1)

                def exps(w, us_):
                    if not full:
                        return
                    for u in us_:
                        j, kk = u // 2, u % 2
                        if u == 0 and (w >= 2 or b.within(1, B - 1)):
                            act.wait_ge(S["pv_done"], b.n * 4 + (w - 1))
                        act.wait_ge(S["scores_ready"], b.n * 32 + (8 * w + u + 1))
                        s.activation(probs[:, w % 2, j, kk, :], sc[u % 2][:, :], ACT.Exp) \
                            .then_inc(S["exp_done"], 1)

                def take_out(bb, gr):
                    act.wait_ge(S["pv_done"], bb.n * 4 + 2 * gr + 2)
                    if bb.within(1, B - 1):
                        act.wait_ge(S["u_ready"], bb.n)
                        act.wait_ge(S["sums_out"], bb.n * 32)
                    s.activation(og[:, gr, :], ob[:, :], ACT.Copy).then_inc(S["og_ready"], 1)

                exps(0, range(0, 1))
                if pv2.within(0, B - 1):
                    act.wait_ge(S["zt_ps"], b.n - 1)
                    if b.within(3, B + 1):
                        act.wait_ge(S["gate_ready"], b.n - 2)
                    s.activation(zt[:, :, :].rearrange("p k t -> p (k t)"), misc[:, :], ACT.Copy) \
                        .then_inc(S["zt_ready"], 1)
                exps(0, range(1, 8))
                if pv.within(0, B - 1):
                    take_out(pv, 1)
                if nb.within(0, B - 1):
                    act.wait_ge(S["vt_ps"], b.n + 2)
                    s.activation(vt[:, nb.parity, :, :, 0:DH], misc[:, :].rearrange("p (k h d) -> p k h d", k=4, h=H),
                                 ACT.Copy).then_inc(S["vt_ready"], 1)
                exps(1, range(0, 5))
                if pv.within(0, B - 1):
                    act.wait_ge(S["u_ready"], b.n)
                    if pv.within(1, B - 1):
                        act.wait_ge(S["t_ready"], b.n - 1)
                    s.activation(us[:, :], misc[:, :], ACT.Copy).then_inc(S["us_ready"], 1)
                exps(1, range(5, 8))
                exps(2, range(8))
                if full:
                    take_out(b, 0)
                exps(3, range(0, 4))
                if behind:
                    act.wait_ge(S["x1_ready"], b.n)
                    s.activation(xres[:, at(xres, pv.n), :].rearrange("p o q -> p (o q)"), x1[:, :], ACT.Copy) \
                        .then_inc(S["x1_kept"], 1)
                exps(3, range(4, 8))

            slots(act, slot)

            act.wait_ge(S["routed"], 1)
            s.activation(gexp[:, :], gdiff[:, :], ACT.Exp).then_inc(S["gexp_ready"], 1)

            def x_high(t, par):
                act.wait_ge(S["xt_ps"], t + 1)
                s.activation(xT[:, par, 0], misc[:, :].rearrange("p (k t) -> p k t", k=KD), ACT.Copy) \
                    .then_inc(S["xt_hi"], 1)

            def tile(t, par, first=False, last=False):
                if not first:
                    act.wait_ge(S["h_ready"], t * 2)
                for n in range(2):
                    act.wait_ge(S["up_ready"], t * 2 + n + 1)
                    s.activation(act_g[:, n * 512:(n + 1) * 512], up[n][0], ACT.Silu).then_inc(S["silu_done"], 1)
                if not last:
                    x_high(t + 1, 1 - par)
                act.wait_ge(S["ht_ps"], t + 1)
                for n in range(2):
                    s.activation(hT[:, par, 0, 4 * n:4 * n + 4, :], hTp[n][:, :].rearrange("p (k t) -> p k t", k=4),
                                 ACT.Copy).then_inc(S["ht_hi"], 1)

            x_high(0, 0)
            tile(0, 0, first=True)
            with act.Fori(0, (T - 3) // 2) as i:
                tile(i * 2 + 1, 1)
                tile(i * 2 + 2, 0)
            tile(T - 2, 1)
            tile(T - 1, 0, last=True)

        @block.vector
        def _(dve):
            v = nc.vector
            v.memset(ks[96:128], 0.0).then_inc(S["rows_set"], 1)
            v.memset(qs[96:128], 0.0).then_inc(S["rows_set"], 1)
            dve.wait_ge(S["rows_set"], 2)
            v.memset(ks[96:98], 1.0).then_inc(S["rows_set"], 1)
            dve.wait_ge(S["ln_ready"], 2)
            v.tensor_scalar(sb_col[:, :], len_ln[:, :], SCALE, None, ALU.mult).then_inc(S["sb_ready"], 1)
            dve.wait_ge(S["consts"], N_CONST)

            def bc_e(col):
                return col.unsqueeze(2).to_broadcast([P, 2, E])

            em = em8[:, :].unsqueeze(1).to_broadcast([P, 2, E])

            def slot(b):
                nb, pv, pv2 = b.plus(1), b.plus(-1), b.plus(-2)

                def maxima(ks_):
                    if not nb.within(0, B - 1):
                        return
                    for k in ks_:
                        if k == 0 and nb.within(2, B - 1):
                            dve.wait_ge(S["mt_ready"], b.n)
                        dve.wait_ge(S["p1_ready"], b.n * 16 + (16 + k + 1))
                        v.tensor_reduce(nm[:, nb.parity, 2 * k:2 * k + 2],
                                        p1[k % 2][:, :].rearrange("p (c k) -> p c k", c=2), AX_X, ALU.max,
                                        negate=True).then_inc(S["p1_used"], 1)

                maxima(range(0, 1))
                if pv2.within(0, B - 1):
                    dve.wait_ge(S["gate_ready"], b.n - 1)
                    v.tensor_copy(gs[:, b.parity, :], misc[:, 0:E]).then_inc(S["gate_copied"], 1)
                maxima(range(1, 2))
                routes = b.parity == 1 and b.within(3, B + 1)
                pair = b.pair - 1
                if routes:
                    st = Steps(dve.wait_ge, S["route_a_steps"], pair, ENGINE_STEPS["route_a"])
                    dve.wait_ge(S["gate_copied"], b.n - 1)
                    src = gs[:, :, :]
                    for a in range(2):
                        best, low = rc[:, 2 * a, :], rc[:, 2 * a + 1, :]
                        st.step(v.tensor_reduce(best, src, AX_X, ALU.max))
                        st.step(v.tensor_tensor(rt[:, 0], src, bc_e(best), ALU.is_equal))
                        st.step(v.tensor_tensor(rt[:, 1], rt[:, 0], em, ALU.mult))
                        st.step(v.tensor_reduce(low, rt[:, 1], AX_X, ALU.min))
                        st.step(v.tensor_tensor(masks[:, a], em, bc_e(low), ALU.is_equal))
                        if a == 0:
                            st.step(v.scalar_tensor_tensor(rt[:, 2], masks[:, 0], -BIG, gs[:, :, :], ALU.mult, ALU.add))
                            src = rt[:, 2]
                        keep = (first_mx, second_mx)[a]
                        st.step(v.tensor_copy(keep[:, bass.ds(pair * 2, 2)], low))
                    st.step(v.tensor_tensor(gdiff[:, bass.ds(pair * 2, 2)], rc[:, 2, :], rc[:, 0, :], ALU.subtract))
                    if b.within(5, B + 1):
                        dve.wait_ge(S["rank_ready"], pair)
                    v.tensor_tensor(maskb[:, :, :], masks[:, 0], masks[:, 1], ALU.add).then_inc(S["mask_ready"], 1)
                    st.end()
                maxima(range(2, 6))
                if pv.within(0, B - 1):
                    dve.wait_ge(S["den_in"], b.n * 16)
                    if pv.within(1, B - 1):
                        dve.wait_ge(S["rec_out"], b.n * 16 - 16)
                    v.reciprocal(rden[:, :], den[:, :]).then_inc(S["rec_ready"], 1)
                maxima(range(6, 9))
                if routes:
                    st = Steps(dve.wait_ge, S["route_b_steps"], pair, ENGINE_STEPS["route_b"])
                    dve.wait_ge(S["mask_ready"], pair + 1)
                    dve.wait_ge(S["rank_ready"], pair + 1)
                    before = misc[:, 0:2 * E].rearrange("p (s e) -> p s e", s=2)
                    st.step(v.tensor_copy(rt[:, 3], misc[:, 2 * E:4 * E].rearrange("p (s e) -> p s e", s=2)))
                    st.step(v.tensor_copy(rt[:, 4], before))
                    v.nop().then_inc(S["rank_used"], 1)
                    pos = rt[:, 4]
                    st.step(v.tensor_tensor(pos, pos, cnt[:, :].unsqueeze(1).to_broadcast([P, 2, E]), ALU.add))
                    st.step(v.tensor_tensor(pos[:, 1, :], pos[:, 1, :], rt[:, 3, 0, :], ALU.add))
                    st.step(v.tensor_tensor(cnt[:, :], cnt[:, :], rt[:, 3, 0, :], ALU.add))
                    st.step(v.tensor_tensor(cnt[:, :], cnt[:, :], rt[:, 3, 1, :], ALU.add))
                    if b.within(5, B + 1):
                        dve.wait_ge(S["slots_out"], pair * 64)
                    for a in range(2):
                        st.step(v.tensor_tensor(rt[:, 5], masks[:, a], pos, ALU.mult))
                        st.step(v.tensor_reduce(rc[:, 6, :], rt[:, 5], AX_X, ALU.add))
                        st.step(v.tensor_copy(rank[:, a, bass.ds(pair * 2, 2)], rc[:, 6, :]))
                        st.step(v.scalar_tensor_tensor(rc[:, 7, :], rc[:, 2 * a + 1, :], float(REG), rc[:, 6, :],
                                                       ALU.mult, ALU.add))
                        st.step(v.tensor_scalar(idx[:, :, a], rc[:, 7, :], float(E * REG), None, ALU.add))
                    st.end()
                    v.nop().then_inc(S["idx_ready"], 1)
                maxima(range(9, 10))
                lb = b.plus(3)
                if lb.within(0, B - 1):
                    dve.wait_ge(loads[lb.parity], lb.pair * 32 + 32)
                    if lb.within(2, B - 1):
                        dve.wait_ge(S["prep_done"], b.n + 2)
                    if lb.within(1, B - 1):
                        dve.wait_ge(S["st1_ready"], b.n + 3)
                    v.bn_stats(st1[:, :], xres[:, at(xres, lb.n), :].rearrange("p o q -> p (o q)")) \
                        .then_inc(S["st1_steps"], 1)
                    dve.wait_ge(S["st1_steps"], b.n + 4)
                    v.nop().then_inc(S["dve_held"], 1)
                    v.bn_aggr(mv1[:, lb.parity, :], st1[:, :]).then_inc(S["st1_ready"], 1)
                maxima(range(10, 14))
                if pv.within(0, B - 1):
                    dve.wait_ge(S["r_ready"], b.n)
                    dve.wait_ge(S["us_ready"], b.n)
                    if pv.within(1, B - 1):
                        dve.wait_ge(S["x1_ready"], b.n - 1)
                    v.tensor_tensor(tb[:, :], misc[:, :], us[:, :], ALU.mult).then_inc(S["t_ready"], 1)
                maxima(range(14, 15))
                if pv.within(0, B - 1):
                    dve.wait_ge(S["x1_ready"], b.n)
                    if pv.within(1, B - 1):
                        dve.wait_ge(S["st2_ready"], b.n - 1)
                    v.bn_stats(st2[:, :], x1[:, :]) \
                        .then_inc(S["st2_steps"], 1)
                    dve.wait_ge(S["st2_steps"], b.n)
                    if pv.within(1, B - 1):
                        dve.wait_ge(S["z_ready"], b.n - 1)
                    v.nop().then_inc(S["dve_held"], 1)
                    v.bn_aggr(mv2[:, :], st2[:, :]).then_inc(S["st2_ready"], 1)
                maxima(range(15, 16))
                if nb.within(0, B - 1):
                    dve.wait_ge(S["mt_ready"], b.n + 2)
                    if nb.within(1, B - 1):
                        dve.wait_ge(S["m_out"], b.n * 16 + 16)
                    v.tensor_copy(mrow[:, 0, :], misc[0:32, 0:P]).then_inc(S["m_steps"], 1)
                    dve.wait_ge(S["m_steps"], b.n + 2)
                    v.tensor_tensor(mrow[:, 1, :], misc[0:32, 0:P], mrow[:, 0, :], ALU.subtract) \
                        .then_inc(S["m_ready"], 1)

            slots(dve, slot)

            done = [1]

            def link(ins):
                done[0] += 1
                ins.then_inc(S["table_chain"], 1)
                dve.wait_ge(S["table_chain"], done[0])

            dve.wait_ge(S["route_b_steps"], ENGINE_STEPS["route_b"] * (B // 2))
            v.nop().then_inc(S["routed"], 1)
            dve.wait_ge(S["table_chain"], 1)
            tiles, cum, tbase, tmp8 = (tl[:, n, :] for n in range(4))
            link(v.tensor_scalar(tl_i[:, :], cnt[:, :], float(P - 1), None, ALU.add))
            link(v.tensor_scalar(tl_i[:, :], tl_i[:, :], 7, None, ALU.logical_shift_right))
            link(v.tensor_copy(tiles, tl_i[:, :]))
            link(v.tensor_copy(cum[:, 0:1], tiles[:, 0:1]))
            for e in range(1, E):
                link(v.tensor_tensor(cum[:, e:e + 1], cum[:, e - 1:e], tiles[:, e:e + 1], ALU.add))
            link(v.tensor_tensor(tbase, cum, tiles, ALU.subtract))
            link(v.tensor_copy(tio[:, :], tio_i[:, :]))
            link(v.scalar_tensor_tensor(tmp8, em8[:, :], float(REG), cnt[:, :], ALU.mult, ALU.add))
            link(v.tensor_scalar(etab[:, 0, :], tmp8, float(E * REG), None, ALU.add))
            link(v.tensor_scalar(etab[:, 1, :], cum, 1.0, None, ALU.add))
            tb3 = tio[:, :].unsqueeze(2).to_broadcast([P, T, E])
            over_t = lambda a: a.unsqueeze(1).to_broadcast([P, T, E])
            expt, used, base_t, row_t, pad_t = (tt[:, n, :] for n in range(5))
            link(v.tensor_tensor(t3[:, :, :], tb3, over_t(cum), ALU.is_ge))
            link(v.tensor_reduce(expt, t3[:, :, :], AX_X, ALU.add))
            link(v.tensor_scalar(used, expt, float(E) - 0.5, None, ALU.is_lt))
            link(v.tensor_scalar(expt, expt, float(E - 1), None, ALU.min))
            link(v.tensor_scalar(base_t, expt, -float(E), None, ALU.add))
            link(v.tensor_tensor(t3[:, :, :], over_t(em8[:, :]), base_t.unsqueeze(2).to_broadcast([P, T, E]), ALU.is_equal))
            link(v.tensor_tensor(t3[:, :, :], t3[:, :, :], over_t(tbase), ALU.mult))
            link(v.tensor_reduce(base_t, t3[:, :, :], AX_X, ALU.add))
            link(v.tensor_tensor(row_t, tio[:, :], base_t, ALU.subtract))
            link(v.tensor_scalar(row_t, row_t, float(P), None, ALU.mult))
            link(v.tensor_tensor(row_t, row_t, used, ALU.mult))
            link(v.tensor_scalar(pad_t, used, -1.0, 1.0, ALU.mult, ALU.add))
            link(v.scalar_tensor_tensor(row_t, pad_t, cnt[:, E - 1:E], row_t, ALU.mult, ALU.add))
            link(v.scalar_tensor_tensor(row_t, expt, float(REG), row_t, ALU.mult, ALU.add))
            link(v.tensor_copy(tab[:, 0, :], row_t))
            link(v.tensor_copy(tab[:, 1, :], expt))
            link(v.tensor_scalar(tab[:, 1, :], tab[:, 1, :], 1, None, ALU.bitwise_and))
            link(v.tensor_scalar(tab[:, 2, :], expt, 1.0, None, ALU.add))
            over_b = lambda a: a.unsqueeze(1).to_broadcast([P, B, E])
            for a, keep in enumerate((first_mx, second_mx)):
                link(v.tensor_tensor(f3, over_b(em8[:, :]), keep[:, :].unsqueeze(2).to_broadcast([P, B, E]),
                                     ALU.is_equal))
                link(v.tensor_tensor(f3, f3, over_b(tbase), ALU.mult))
                link(v.tensor_reduce(ff[:, :], f3, AX_X, ALU.add))
                link(v.scalar_tensor_tensor(fidx[:, a, :], ff[:, :], float(P), rank[:, a, :], ALU.mult, ALU.add))
            dve.wait_ge(S["vt_ps"], B)
            link(v.memset(cv[:, :], 0.0))
            v.nop().then_inc(S["tab_ready"], 1)
            dve.wait_ge(S["gexp_ready"], 1)
            link(v.tensor_scalar(gsum[:, :], gexp[:, :], 1.0, None, ALU.add))
            link(v.reciprocal(gate[:, 0, :], gsum[:, :]))
            link(v.tensor_tensor(gate[:, 1, :], gexp[:, :], gate[:, 0, :], ALU.mult))

            def x_low(t, par):
                dve.wait_ge(S["xt_hi"], t + 1)
                v.tensor_tensor(xT[:, par, 1], misc[:, :].rearrange("p (k t) -> p k t", k=KD), xT[:, par, 0],
                                ALU.subtract).then_inc(S["xt_lo"], 1)

            def take_y(t, par, early=False):
                dve.wait_ge(S["tiles_done"], t + 2)
                if not early:
                    dve.wait_ge(y_out[par], (t - par) * 8)
                v.tensor_copy(yb[:, par, :], ob[:, :]).then_inc(S["yb_ready"], 1)

            def tile(t, par, first=False, last=False, early=False):
                if not first:
                    dve.wait_ge(S["ht_ps"], t)
                for n in range(2):
                    dve.wait_ge(S["silu_done"], t * 2 + n + 1)
                    v.tensor_tensor(hbuf[:, n * 512:(n + 1) * 512], up[n][1], act_g[:, n * 512:(n + 1) * 512],
                                    ALU.mult).then_inc(S["h_ready"], 1)
                if not last:
                    x_low(t + 1, 1 - par)
                if not first:
                    take_y(t - 1, 1 - par, early)
                for n in range(2):
                    dve.wait_ge(S["ht_hi"], t * 2 + n + 1)
                    v.tensor_tensor(hT[:, par, 1, 4 * n:4 * n + 4, :], hTp[n][:, :].rearrange("p (k t) -> p k t", k=4),
                                    hT[:, par, 0, 4 * n:4 * n + 4, :], ALU.subtract).then_inc(S["ht_lo"], 1)

            x_low(0, 0)
            tile(0, 0, first=True)
            tile(1, 1, early=True)
            tile(2, 0, early=True)
            with dve.Fori(1, (T - 3) // 2) as i:
                tile(i * 2 + 1, 1)
                tile(i * 2 + 2, 0)
            tile(T - 2, 1)
            tile(T - 1, 0, last=True)
            take_y(T - 1, 0)

            v.nop().then_inc(S["comb_steps"], 1)
            with dve.Fori(0, B // 4) as i:
                for r in range(4):
                    b = i * 4 + r
                    dve.wait_ge(g_in[r], i * 32 + 32)
                    xr = xres[:, bass.ds(b, 1), :].rearrange("p o q -> p (o q)")
                    v.scalar_tensor_tensor(xr, gb[:, r, 0, :], gate[:, 0, bass.ds(b, 1)], xr, ALU.mult, ALU.add) \
                        .then_inc(S["comb_steps"], 1)
                    dve.wait_ge(S["comb_steps"], b + 2)
                    v.scalar_tensor_tensor(xr, gb[:, r, 1, :], gate[:, 1, bass.ds(b, 1)], xr, ALU.mult, ALU.add) \
                        .then_inc(S["comb_done"], 1)

        @block.tensor
        def _(pe):
            m = nc.tensor
            pe.wait_ge(S["consts"], N_CONST)
            pe.wait_ge(S["rows_set"], 3)
            pe.wait_ge(S["gate_in"], 16)

            P1_PLAN = {(0, 0): 1, (0, 2): 1, (0, 3): 1, (0, 5): 1, (0, 6): 1,
                       (1, 0): 1, (1, 1): 1, (1, 3): 1, (1, 4): 1, (1, 6): 1,
                       (2, 0): 1, (2, 2): 1, (2, 3): 1, (2, 5): 1, (2, 6): 1, (3, 0): 1}

            def slot(b):
                nb, pv, pv2 = b.plus(1), b.plus(-1), b.plus(-2)
                full, ahead = b.within(0, B - 1), nb.within(0, B - 1)
                behind = pv.within(0, B - 1)
                done = [0]

                def rows_unit():
                    k = done[0]
                    done[0] += 1
                    hh, qh = k // 2, k % 2
                    if k % 8 == 0:
                        pe.wait_ge(st_in[nb.parity][k // 8], nb.pair * 192 + 192)
                    if k >= 2 or nb.within(1, B - 1):
                        pe.wait_ge(S["p1_used"], b.n * 16 + (16 + k - 1))
                    for c in range(2):
                        q0 = (2 * qh + c) * P
                        ins = m.matmul(p1[k % 2][:, c * 512:(c + 1) * 512], qs[0:KROWS, nb.parity, hh, q0:q0 + P],
                                       ks[0:KROWS, nb.parity, hh, :], start=True, stop=True)
                    ins.then_inc(S["p1_ready"], 1)

                def score(w, u):
                    j, kk = u // 2, u % 2
                    h, kc = 4 * (w // 2) + j, 2 * (w % 2) + kk
                    if w == 0 and u == 0:
                        pe.wait_ge(S["m_in"], b.n * 16 + 16)
                    if w or u >= 2 or b.within(1, B - 1):
                        pe.wait_ge(S["exp_done"], b.n * 32 + (8 * w + u - 1))
                    m.matmul(sc[u % 2][:, :], ks[:, b.parity, h, kc * P:(kc + 1) * P], qs[:, b.parity, h, :],
                             start=True, stop=True).then_inc(S["scores_ready"], 1)

                def values(bb, w, kk):
                    if kk == 0:
                        pe.wait_ge(S["exp_done"], bb.n * 32 + 8 * (w + 1))
                        if w == 0:
                            pe.wait_ge(S["vt_ready"], bb.n + 1)
                        if w == 2 or (w == 0 and bb.within(1, B - 1)):
                            pe.wait_ge(S["og_ready"], bb.n * 2 + w // 2)
                    kc = 2 * (w % 2) + kk
                    for j in range(4):
                        ins = m.matmul(ob[32 * j:32 * j + 32, :], vt[:, bb.parity, kc, 4 * (w // 2) + j, :],
                                       probs[:, w % 2, j, kk, :], start=(kc == 0), stop=(kc == 3))
                    if kk == 1:
                        ins.then_inc(S["pv_done"], 1)

                reader = (S["zt_ready"], b.n - 1) if pv2.within(0, B - 1) else \
                    (S["m_ready"], b.n + 1) if full else None

                for w in range(4):
                    for u in range(8):
                        if ahead and (w, u) in P1_PLAN:
                            rows_unit()
                        if full:
                            score(w, u)
                        if (w, u) == (0, 3) and pv2.within(0, B - 1):
                            pe.wait_ge(*reader)
                            for k in range(KD):
                                ins = m.matmul(misc[:, 0:E], zt[:, k, :], gw[:, k, :], start=(k == 0),
                                               stop=(k == KD - 1))
                            ins.then_inc(S["gate_ready"], 1)
                            reader = (S["gate_copied"], b.n - 1)
                        if u in (3, 6):
                            kk = 0 if u == 3 else 1
                            if w == 0 and behind:
                                values(pv, 3, kk)
                            if w > 0 and full:
                                values(b, w - 1, kk)
                        if (w, u) == (0, 7) and ahead:
                            pe.wait_ge(S["cv_in"], b.n * 16 + 32)
                            if reader:
                                pe.wait_ge(*reader)
                            for kc in range(4):
                                ins = m.transpose(misc[:, kc * P:(kc + 1) * P], cv[:, kc * P:(kc + 1) * P], ident[:, :])
                            ins.then_inc(S["vt_ps"], 1)
                            reader = (S["vt_ready"], b.n + 2)
                        if (w, u) == (1, 2) and behind:
                            if reader:
                                pe.wait_ge(*reader)
                            pe.wait_ge(S["og_ready"], b.n * 2)
                            for gr in range(2):
                                ins = m.matmul(misc[:, :], selu[:, gr, :], og[:, gr, :], start=(gr == 0), stop=(gr == 1))
                            ins.then_inc(S["u_ready"], 1)
                            reader = (S["us_ready"], b.n)
                        if (w, u) == (1, 6) and b.parity == 1 and b.within(3, B + 1):
                            pe.wait_ge(*reader)
                            pe.wait_ge(S["mask_ready"], b.pair)
                            mb = maskb[:, :, :].rearrange("p s e -> p (s e)")
                            m.matmul(misc[:, 0:2 * E], ltri[:, :], mb, start=True, stop=True)
                            m.matmul(misc[:, 2 * E:4 * E], onesb[:, :], mb, start=True, stop=True) \
                                .then_inc(S["rank_ready"], 1)
                            reader = (S["rank_used"], b.pair)
                        if (w, u) == (2, 6) and behind:
                            pe.wait_ge(S["rec_in"], b.n * 16)
                            pe.wait_ge(*reader)
                            m.matmul(misc[:, :], selb[:, :], r8[:, :], start=True, stop=True).then_inc(S["r_ready"], 1)
                            reader = (S["t_ready"], b.n)
                        if (w, u) == (3, 3) and ahead:
                            pe.wait_ge(S["p1_used"], b.n * 16 + 32)
                            pe.wait_ge(*reader)
                            m.transpose(misc[:, 0:P], nm[:, nb.parity, :], ident[:, :]).then_inc(S["mt_ready"], 1)
                            reader = (S["m_ready"], b.n + 2)
                        if (w, u) == (3, 6) and behind:
                            pe.wait_ge(S["z_ready"], b.n)
                            pe.wait_ge(*reader)
                            for k in range(KD):
                                ins = m.transpose(misc[:, k * P:(k + 1) * P], z[:, pv.parity, k * P:(k + 1) * P],
                                                  ident[:, :])
                            ins.then_inc(S["zt_ps"], 1)

            slots(pe, slot)
            pe.wait_ge(S["og_ready"], 2 * B)
            m.nop().then_inc(S["attn_done"], 1)

            pe.wait_ge(S["tab_ready"], 1)
            m.nop().then_inc(S["tiles_done"], 1)

            def x_tile(t, par, first=False):
                pe.wait_ge(xrow_in[par], (t - par) * 8 + 16)
                if not first:
                    pe.wait_ge(S["xt_lo"], t)
                for k in range(KD):
                    ins = m.transpose(misc[:, k * P:(k + 1) * P], xrow[:, par, k * P:(k + 1) * P], ident[:, :])
                ins.then_inc(S["xt_ps"], 1)

            def split_products(bank, stat, w_off, n_chunks, stride, col):
                for k in range(n_chunks):
                    for n, (s_part, w_part) in enumerate(((0, 0), (0, 1), (1, 0))):
                        at_w = w_off + (w_part * WLEN + col + k * stride)
                        ins = m.matmul(bank, stat[:, s_part, k, :], W[:, bass.ds(at_w, 512)],
                                       start=(k == 0 and n == 0), stop=(k == n_chunks - 1 and n == 2))
                return ins

            def half_of(t):
                e = pe.value_load(tab[0:1, 1, bass.ds(t, 1)], min_val=0, max_val=1)
                return e * half

            def up_tile(t, par, first=False):
                ready = pe.value_load(tab[0:1, 2, bass.ds(t, 1)], min_val=1, max_val=E)
                off = half_of(t)
                pe.wait_ge(S["w_ready"], ready)
                pe.wait_ge(S["xt_lo"], t + 1)
                for n in range(2):
                    if not first:
                        pe.wait_ge(S["h_ready"], t * 2 - 1 + n)
                    for wn in range(2):
                        ins = split_products(up[n][wn], xT[:, par], off, KD, I, wn * KD * I + n * 512)
                    ins.then_inc(S["up_ready"], 1)

            def down_tile(t, par, first=False):
                off = half_of(t)
                pe.wait_ge(S["ht_lo"], t * 2 + 2)
                if not first:
                    pe.wait_ge(S["yb_ready"], t)
                ins = split_products(ob[:, :], hT[:, par], off, KI, D, 2 * KD * I)
                ins.then_inc(S["tiles_done"], 1)

            def h_tile(t, par, first=False):
                pe.wait_ge(S["h_ready"], t * 2 + 2)
                if not first:
                    pe.wait_ge(S["ht_lo"], t * 2)
                for k in range(KI):
                    ins = m.transpose(hTp[k // 4][:, (k % 4) * P:(k % 4 + 1) * P], hbuf[:, k * P:(k + 1) * P], ident[:, :])
                ins.then_inc(S["ht_ps"], 1)

            def tile(t, par, last=False, second=False):
                up_tile(t, par)
                if not last:
                    x_tile(t + 1, 1 - par)
                down_tile(t - 1, 1 - par, first=second)
                h_tile(t, par)

            x_tile(0, 0, first=True)
            up_tile(0, 0, first=True)
            x_tile(1, 1)
            h_tile(0, 0, first=True)
            tile(1, 1, second=True)
            tile(2, 0)
            with pe.Fori(1, (T - 3) // 2) as i:
                tile(i * 2 + 1, 1)
                tile(i * 2 + 2, 0)
            tile(T - 2, 1)
            tile(T - 1, 0, last=True)
            down_tile(T - 1, 0)


def kernel(x, ctx_2048, itok_B_779_1933, L0_ffn_gate_w, L0_ffn_w1, L0_ffn_w2, L0_ffn_w3):
    import concourse.bacc as _bacc
    from concourse.bass_utils import run_bass_kernel_spmd as _run

    def chunked(w):
        w = np.asarray(w)
        e, o, i = w.shape
        return w.transpose(0, 2, 1).reshape(e, i // P, P, o).transpose(0, 2, 1, 3).reshape(e, P, i // P * o)

    arrays = {
        "x_dram": np.ascontiguousarray(x),
        "ctx_dram": np.ascontiguousarray(ctx_2048),
        "lengths_dram": np.ascontiguousarray(itok_B_779_1933),
        "wpack_dram": np.ascontiguousarray(np.concatenate(
            [chunked(L0_ffn_w1), chunked(L0_ffn_w3), chunked(L0_ffn_w2)], axis=2)),
        "gate_dram": np.ascontiguousarray(np.asarray(L0_ffn_gate_w).T),
    }
    nc = _bacc.Bacc("TRN2", target_bir_lowering=False, num_devices=1)
    args = [nc.dram_tensor(n, a.shape, mybir.dt.from_np(a.dtype), kind="ExternalInput").ap() for n, a in arrays.items()]
    out = nc.dram_tensor("out_dram", arrays["x_dram"].shape, F32, kind="ExternalOutput").ap()
    build(nc, *args, out)
    r = _run(nc, [arrays], core_ids=[0])
    return r.results[0]["out_dram"]
```

```python
from contextlib import ExitStack

import numpy as np

import concourse.bass as bass
from concourse import mybir

ALU = mybir.AluOpType
ACT = mybir.ActivationFunctionType
F32 = mybir.dt.float32
BF16 = mybir.dt.bfloat16
I32 = mybir.dt.int32
U32 = mybir.dt.uint32
AX_X = mybir.AxisListType.X

P = 128
LOOP_FIRST, LOOP_LAST = 2, 6
LEAD = 5
ENGINE_STEPS = {"prep": 14, "z": 4, "route_a": 6, "route_b": 5}


class Batch:

    def __init__(self, pair, parity, low, high):
        self.pair, self.parity = pair, parity
        self.low, self.high = low, high

    @property
    def n(self):
        return self.pair * 2 + self.parity

    def plus(self, k):
        p = self.parity + k
        return Batch(self.pair + p // 2, p % 2, self.low + k, self.high + k)

    def within(self, first, last):
        inside = first <= self.low and self.high <= last
        assert inside or self.high < first or self.low > last
        return inside


class Steps:

    def __init__(self, wait, sem, index, each):
        self.wait, self.sem, self.index, self.each, self.done = wait, sem, index, each, 0

    def step(self, instruction):
        self.done += 1
        instruction.then_inc(self.sem, 1)
        self.wait(self.sem, self.index * self.each + self.done)

    def end(self):
        assert self.done == self.each, (self.done, self.each)


def build(nc, x, ctx_kv, lengths, wpack, gate_t, out):
    B, HD, L = x.shape
    LK = ctx_kv.shape[2]
    H = 8
    DH = HD // H
    E, _, WLEN = wpack.shape
    D = L
    I = WLEN // (3 * D // P)
    KD, KI = D // P, I // P
    assert WLEN == KD * I * 2 + KI * D and HD == P and L == LK == 512
    SCALE = 1.0 / (64 ** 0.5 * float(np.log(20)))
    EPS = 1e-5
    TOK = B * P
    REG = TOK + P
    T = (2 * TOK + E * (P - 1)) // P
    CH = 1024
    NCH = WLEN // CH
    KROWS, MROW = 6 * DH, 6 * DH

    pd = nc.dram_tensor("parts_dram", [B, 2, P, 6, L], BF16, kind="Internal").ap()
    zs = nc.dram_tensor("slots_dram", [E * REG, D], F32, kind="Internal").ap()
    ys = nc.dram_tensor("expert_out_dram", [T * P, D], F32, kind="Internal").ap()
    sums_dram = nc.dram_tensor("sums_dram", [B, H, L], F32, kind="Internal").ap()
    recips_dram = nc.dram_tensor("recips_dram", [B, H, L], F32, kind="Internal").ap()
    maxima_dram = nc.dram_tensor("maxima_dram", [B, 2, H * L], BF16, kind="Internal").ap()

    with ExitStack() as cx:
        def sb(name, shape, dt):
            return cx.enter_context(nc.sbuf_tensor(name, shape, dt))

        def pb(name, shape, dt=F32):
            return cx.enter_context(nc.psum_tensor(name, shape, dt))

        def sem(name):
            return cx.enter_context(nc.semaphore(name))

        xres = sb("xres", [P, B, L], F32)
        W = sb("W", [P, 2 * 2 * WLEN], BF16)
        stage = sb("stage", [P, 2, CH], F32)
        ident = sb("ident", [P, P], F32)
        numbers = sb("numbers", [P, E], F32)
        first_rows = sb("first_rows", [P, E], F32)
        scores2 = sb("scores2", [P, B, 2], F32)
        experts2 = sb("experts2", [P, B, 2], F32)
        rows = sb("rows", [P, B, 2], F32)

        half = 2 * WLEN
        probs = W[:, half:half + 16384].bitcast(F32).rearrange("p (b j k q) -> p b j k q", b=2, j=4, k=2)
        ks = W[:, half + 16384:half + 24576].rearrange("p (b h k) -> p b h k", b=2, h=H)
        U = sb("U", [P, 11264], F32)
        qs = U[:, 0:4096].bitcast(BF16).rearrange("p (b h q) -> p b h q", b=2, h=H)
        parts = U[:, 4096:7168].bitcast(BF16).rearrange("p (b c q) -> p b c q", b=2, c=6)
        vt = U[:, 7168:9216].rearrange("p (b k h c) -> p b k h c", b=2, k=4, h=H)
        cin = U[:, 9216:10240].rearrange("p (b k) -> p b k", b=2)
        og = U[:, 10240:11264].rearrange("p (g q) -> p g q", g=2)
        cv = sb("cv", [P, LK], F32)
        norm = sb("norm", [P, L], F32)
        rest = sb("rest", [P, L], F32)
        us = sb("us", [P, L], F32)
        tb = sb("tb", [P, L], F32)
        x1 = sb("x1", [P, L], F32)
        z = sb("z", [P, 2, D], F32)
        zt = sb("zt", [P, KD, P], F32)
        selu = sb("selu", [P, 2, P], F32)
        selb = sb("selb", [8, P], F32)
        r8 = sb("r8", [8, L], F32)
        den = sb("den", [P, 32], F32)
        rden = sb("rden", [P, 32], F32)
        nm = sb("nm", [P, 2, P], F32)
        mrow = sb("mrow", [32, 2, P], BF16)
        len_i = sb("len_i", [P, B], I32)
        len_f = sb("len_f", [P, B], F32)
        sb_col = sb("sb_col", [P, B], F32)
        st1 = sb("st1", [P, 6], F32)
        mv1 = sb("mv1", [P, 2, 2], F32)
        st2 = sb("st2", [P, 6], F32)
        mv2 = sb("mv2", [P, 2], F32)
        mhalf = sb("mhalf", [P, 1], F32)
        zero = sb("zero", [P, 1], F32)
        psc = sb("psc", [P, 4], F32)
        zsc = sb("zsc", [P, 4], F32)
        gw = sb("gw", [P, KD, E], F32)
        sorted8 = sb("sorted8", [P, E], F32)
        order8 = sb("order8", [P, E], U32)
        masks = sb("masks", [P, 2, E], F32)
        place = sb("place", [P, 3, E], F32)
        maskb = sb("maskb", [P, E], BF16)
        mask_sum = sb("mask_sum", [P, E], BF16)
        ltri = sb("ltri", [P, P], BF16)
        onesb = sb("onesb", [P, P], BF16)
        idx = sb("idx", [P, 2, 2], I32)
        tio_i = sb("tio_i", [P, T], I32)
        tio = sb("tio", [P, 2, T], F32)
        upto = sb("upto", [P, E, E], F32)
        tab = sb("tab", [P, 3, T], I32)
        etab = sb("etab", [P, 2, E], I32)
        fidx = sb("fidx", [P, B, 2], I32)
        gexp = sb("gexp", [P, B], F32)
        gate = sb("gate", [P, 2, B], F32)
        small = U[:, 8192:9216]
        t3 = U[:, 7168:7168 + T * (E - 1)].rearrange("p (t e) -> p t e", e=E - 1)
        c3 = U[:, 7680:7680 + 2 * B * E].rearrange("p (n e) -> p n e", e=E)
        k3 = U[:, 7936:7936 + E * B].rearrange("p (e k) -> p e k", k=B)
        tiles, cum, tbase, base, delta, zero_rows, total = (small[:, n * E:(n + 1) * E] for n in range(7))
        expt, row_t = small[:, 128:128 + T], small[:, 192:192 + T]
        at_base = small[:, 256:256 + 2 * B]

        xrow = U[:, 0:1024].rearrange("p (b d) -> p b d", b=2)
        xT = U[:, 1024:2048].bitcast(BF16).rearrange("p (b s k t) -> p b s k t", b=2, s=2, k=KD)
        act_g = U[:, 2048:3072]
        hbuf = U[:, 3072:4096]
        hT = U[:, 4096:6144].bitcast(BF16).rearrange("p (b s k t) -> p b s k t", b=2, s=2, k=KI)
        yb = U[:, 6144:7168].rearrange("p (b d) -> p b d", b=2)
        gb = U[:, 7168:11264].rearrange("p (b a d) -> p b a d", b=4, a=2)

        sc = [pb(f"scores{i}", [P, 512]) for i in range(2)]
        p1 = [pb(f"rows{i}", [P, 1024]) for i in range(2)]
        ob = pb("heads_out", [P, 512])
        misc = pb("misc", [P, 512])
        up = [[p1[0][:, 0:512], p1[1][:, 0:512]], [p1[0][:, 512:1024], p1[1][:, 512:1024]]]
        hTp = [sc[0], sc[1]]

        names = """setup numbered consts rows_set gate_in len_in ln_ready sb_ready chain table_chain prep_steps z_steps
            route_a_steps route_b_steps pd_out sums_out rec_out m_out den_in rec_in m_in cv_in p1_ready p1_used scores_ready
            exp_done pv_done og_ready vt_ps vt_ready u_ready us_ready r_ready t_ready x1_ready x1_kept zt_ps zt_ready
            gate_ready gate_used mask_ready rank_ready rank_used idx_ready rec_ready st1_steps
            st2_steps st1_ready st2_ready prep_done z_ready mt_ready m_steps m_ready chunk_steps w_ready
            tab_ready zero_out tiles_done xt_ps xt_hi xt_lo up_ready silu_done h_ready ht_ps ht_hi ht_lo
            yb_ready pool_held dve_held sp_held gexp_ready gate_w_ready comb_steps comb_done out_done attn_done routed cnt_ready zero_ready""".split()
        S = {n: sem(n) for n in names}
        loads = [sem(f"loads{i}") for i in range(2)]
        st_in = [[sem(f"stack{i}{j}") for j in range(2)] for i in range(2)]
        slots_out = [sem(f"slots_out{i}") for i in range(2)]
        w_in = [sem(f"w_in{i}") for i in range(2)]
        xrow_in = [sem(f"xrow_in{i}") for i in range(2)]
        y_out = [sem(f"y_out{i}") for i in range(2)]
        g_in = [sem(f"g_in{i}") for i in range(4)]

        def slots(engine, body):
            for b in range(-3, 2 * LOOP_FIRST):
                body(Batch(b // 2, b % 2, b, b))
            with engine.Fori(LOOP_FIRST, LOOP_LAST) as i:
                for par in range(2):
                    body(Batch(i, par, 2 * LOOP_FIRST + par, 2 * LOOP_LAST - 2 + par))
            for b in range(2 * LOOP_LAST, B + 2):
                body(Batch(b // 2, b % 2, b, b))

        N_CONST = 10
        block = cx.enter_context(nc.Block())

        @block.sync
        def _(sp):
            sp.dma_start(len_i[:, :], lengths.partition_broadcast(P)).then_inc(S["len_in"], 16)
            sp.dma_start(gw[:, :, :], gate_t.rearrange("(k p) e -> p k e", p=P)).then_inc(S["gate_in"], 16)
            sp.wait_ge(S["consts"], N_CONST)

            def reload(b, half_h):
                heads = slice(4 * half_h, 4 * half_h + 4)
                for n, stacked in enumerate((qs, ks)):
                    sp.dma_start(stacked[0:KROWS, b.parity, heads, :],
                                 pd[bass.ds(b.n, 1), n, 4 * DH * half_h:4 * DH * (half_h + 1)].rearrange(
                                     "o (h d) c q -> (o d c) h q", h=4)).then_inc(st_in[b.parity][half_h], 16)

            def store_parts(b, n):
                dst = pd[bass.ds(b.n, 1), n].rearrange("o p c q -> (o p) c q")
                src = parts[:, b.parity]
                for first, count, part in ((0, 3, 0), (3, 2, 1), (5, 1, 2)):
                    values = src[:, 0:count, :] if n == 0 else \
                        src[:, 3 + part:4 + part, :].to_broadcast([P, count, L])
                    sp.dma_start(dst[:, first:first + count, :], values).then_inc(S["pd_out"], 16)

            def slot(b):
                nb = b.plus(1)
                if nb.within(0, B - 1):
                    if b.within(1, B):
                        sp.wait_ge(S["scores_ready"], b.n * 32)
                    reload(nb, 1)
                lb = b.plus(3)
                if lb.within(0, B - 1):
                    if b.within(-1, B):
                        sp.wait_ge(S["prep_done"], b.n + 2)
                    sp.dma_start(xres[:, bass.ds(lb.n, 1), :], x[bass.ds(lb.n, 1)].rearrange("o p q -> p o q")) \
                        .then_inc(loads[lb.parity], 16)
                    sp.dma_start(cin[:, lb.parity, :], ctx_kv[bass.ds(lb.n, 1)].rearrange("o p q -> p (o q)")) \
                        .then_inc(loads[lb.parity], 16)
                pv, pbt = b.plus(-1), b.plus(2)
                behind, ahead2 = pv.within(0, B - 1), pbt.within(0, B - 1)
                if ahead2:
                    sp.wait_ge(S["prep_steps"], (b.n + 2) * ENGINE_STEPS["prep"] + 10)
                    store_parts(pbt, 0)
                if behind:
                    sp.wait_ge(S["og_ready"], b.n * 2)
                    for g in range(2):
                        sp.dma_start(sums_dram[bass.ds(pv.n, 1), 4 * g:4 * g + 4].rearrange("o h q -> (o h) q"),
                                     og[16:113:32, g, :]).then_inc(S["sums_out"], 16)
                    sp.wait_ge(S["sums_out"], b.n * 32)
                    sp.dma_start(den[:, :], sums_dram[bass.ds(pv.n, 1)].rearrange("o h (p f) -> (o h p) f", f=32)) \
                        .then_inc(S["den_in"], 16)
                if ahead2:
                    sp.wait_ge(S["prep_done"], b.n + 3)
                    store_parts(pbt, 1)
                if behind:
                    sp.wait_ge(S["rec_ready"], b.n)
                    sp.dma_start(recips_dram[bass.ds(pv.n, 1)].rearrange("o h (p f) -> (o h p) f", f=32),
                                 rden[:, :]).then_inc(S["rec_out"], 16)
                if ahead2:
                    sp.wait_ge(S["pd_out"], b.n * 96 + 288)
                    sp.nop().then_inc(S["sp_held"], 1)
                    if b.within(0, B - 1):
                        sp.wait_ge(S["scores_ready"], b.n * 32 + 16)
                    reload(pbt, 0)
                if behind:
                    sp.wait_ge(S["rec_out"], b.n * 16)
                    sp.nop().then_inc(S["sp_held"], 1)
                    if b.within(2, B):
                        sp.wait_ge(S["r_ready"], b.n - 1)
                    sp.dma_start(r8[:, :], recips_dram[bass.ds(pv.n, 1)].rearrange("o h q -> (o h) q")) \
                        .then_inc(S["rec_in"], 16)
                if nb.within(0, B - 1):
                    sp.wait_ge(S["m_ready"], b.n + 2)
                    sp.dma_start(maxima_dram[bass.ds(nb.n, 1)].rearrange("o s (c q) -> c (o s) q", q=P),
                                 mrow[:, :, :]).then_inc(S["m_out"], 16)
                    sp.wait_ge(S["m_out"], b.n * 16 + 32)
                    sp.dma_start(qs[MROW:MROW + 2, nb.parity],
                                 maxima_dram[bass.ds(nb.n, 1)].rearrange("o s (h q) -> (o s) h q", h=H)) \
                        .then_inc(S["m_in"], 16)
                if pbt.within(0, B - 1):
                    if nb.within(0, B - 1):
                        sp.wait_ge(S["vt_ps"], b.n + 2)
                    sp.dma_start(cv[:, :], ctx_kv[bass.ds(pbt.n, 1)].rearrange("o p q -> p (o q)")) \
                        .then_inc(S["cv_in"], 16)

            slots(sp, slot)

            sp.wait_ge(S["zero_ready"], 1)
            for e in range(E):
                r = sp.value_load(etab[0:1, 0, e:e + 1], min_val=0, max_val=E * REG - P)
                sp.dma_start(zs[bass.ds(r, P), :], cv[:, :]).then_inc(S["zero_out"], 16)
            sp.wait_ge(S["zero_out"], 16 * E)
            for i in range(2):
                sp.wait_ge(slots_out[i], 32 * (B // 2))
            sp.wait_ge(S["tab_ready"], 1)

            def load_tile(t, par):
                r = sp.value_load(tab[0:1, 0, bass.ds(t, 1)], min_val=0, max_val=E * REG - P)
                sp.dma_start(xrow[:, par, :], zs[bass.ds(r, P), :]).then_inc(xrow_in[par], 16)

            def store_tile(t, par):
                sp.wait_ge(S["yb_ready"], t + 1)
                sp.dma_start(ys[bass.ds(t * P, P), :], yb[:, par, :]).then_inc(y_out[par], 16)

            load_tile(0, 0)
            load_tile(1, 1)
            with sp.Fori(0, (T - 3) // 2) as i:
                for par in range(2):
                    sp.wait_ge(S["xt_ps"], i * 2 + par + 1)
                    load_tile(i * 2 + par + 2, par)
                    store_tile(i * 2 + par, par)
            sp.wait_ge(S["xt_ps"], T - 2)
            load_tile(T - 1, 0)
            store_tile(T - 3, 0)
            store_tile(T - 2, 1)
            store_tile(T - 1, 0)

            with sp.Fori(0, B) as b:
                sp.wait_ge(S["comb_done"], b + 1)
                sp.dma_start(out[bass.ds(b, 1)].rearrange("o p d -> p o d"), xres[:, bass.ds(b, 1), :]) \
                    .then_inc(S["out_done"], 16)
            sp.wait_ge(S["out_done"], 16 * B)

        @block.gpsimd
        def _(pool):
            g = nc.gpsimd

            def hold(semaphore, value):
                pool.wait_ge(semaphore, value)
                g.nop().then_inc(S["pool_held"], 1)

            k = S["setup"]
            g.memset(ident[:, :], 0.0).then_inc(k, 1)
            g.memset(selu[:, :, :], 0.0).then_inc(k, 1)
            g.memset(selb[:, :], 0.0).then_inc(k, 1)
            g.memset(ltri[:, :], 1.0).then_inc(k, 1)
            g.memset(vt, 0.0).then_inc(k, 1)
            hold(k, 5)
            c = S["consts"]
            g.affine_select(out=ident[:, :], in_=ident[:, :], compare_op=ALU.not_equal, fill=1.0, base=0,
                            pattern=[[-1, P]], channel_multiplier=1).then_inc(c, 1)
            for gr in range(2):
                v = selu[:, gr, :].rearrange("p (h d) -> p h d", h=H)
                g.affine_select(out=v, in_=v, compare_op=ALU.not_equal, fill=1.0, base=128 * gr,
                                pattern=[[-32, H], [-1, DH]], channel_multiplier=1).then_inc(c, 1)
            v = selb[:, :].rearrange("p (h d) -> p h d", h=H)
            g.affine_select(out=v, in_=v, compare_op=ALU.not_equal, fill=1.0, base=0,
                            pattern=[[-1, H], [0, DH]], channel_multiplier=1).then_inc(c, 1)
            g.affine_select(out=ltri[:, :], in_=ltri[:, :], compare_op=ALU.is_gt, fill=0.0, base=0,
                            pattern=[[1, P]], channel_multiplier=-1).then_inc(c, 1)
            g.memset(onesb[:, :], 1.0).then_inc(c, 1)
            g.memset(vt[:, :, :, :, DH:DH + 1], 1.0).then_inc(c, 1)
            g.memset(nm[:, :, :], 0.0).then_inc(c, 1)
            g.memset(mhalf[:, :], -0.5).then_inc(c, 1)
            g.memset(zero[:, :], 0.0).then_inc(c, 1)
            g.iota(tio_i[:, :], pattern=[[1, T]], base=0, channel_multiplier=0).then_inc(S["numbered"], 1)
            hold(c, N_CONST)

            def high_low(steps, dst_hi, dst_lo, src, tmp=None, moving=False):
                if moving:
                    steps.step(g.tensor_tensor(dst_hi, src, zero[:, :].to_broadcast(src.shape), ALU.add))
                else:
                    steps.step(g.tensor_scalar(dst_hi, src, 1.0, 0.0, ALU.mult, ALU.add))
                steps.step(g.tensor_tensor(tmp if tmp is not None else dst_lo, src, dst_hi, ALU.subtract))

            def split_chunk(dst_half, col, n, n_pair, par, moving=False):
                steps = Steps(hold, S["chunk_steps"], n, 2)
                hold(w_in[par], n_pair * 16 + 16)
                base = dst_half * half
                high_low(steps, W[:, bass.ds(col + base, CH)], W[:, bass.ds(col + (base + WLEN), CH)],
                         stage[:, par, :], moving=moving)
                steps.end()

            def slot(b):
                pbt = b.plus(2)
                if pbt.within(0, B - 1):
                    st = Steps(hold, S["prep_steps"], pbt.n, ENGINE_STEPS["prep"])
                    hold(S["st1_ready"], b.n + 3)
                    if pbt.within(0, 0):
                        hold(S["sb_ready"], 1)
                    if pbt.within(2, B - 1):
                        hold(S["pd_out"], b.n * 96 + 96)
                    mean, var = mv1[:, pbt.parity, 0:1], mv1[:, pbt.parity, 1:2]
                    st.step(g.tensor_scalar(psc[:, 0:1], var, EPS, 1.0, ALU.add, ALU.mult))
                    st.step(g.tensor_tensor(psc[:, 1:2], psc[:, 0:1], mhalf[:, :], ALU.pow))
                    st.step(g.tensor_tensor(psc[:, 2:3], psc[:, 1:2], sb_col[:, bass.ds(pbt.n, 1)], ALU.mult))
                    st.step(g.tensor_scalar(psc[:, 3:4], mean, -1.0, 0.0, ALU.mult, ALU.add))
                    st.step(g.tensor_tensor(norm[:, :], xres[:, bass.ds(pbt.n, 1), :].rearrange("p o q -> p (o q)"),
                                            psc[:, 3:4].to_broadcast([P, L]), ALU.add))
                    st.step(g.tensor_scalar(norm[:, :], norm[:, :], psc[:, 2:3], 0.0, ALU.mult, ALU.add))
                    pt = parts[:, pbt.parity]
                    for c0, src in ((0, norm[:, :]), (3, cin[:, pbt.parity, :])):
                        high_low(st, pt[:, c0, :], None, src, rest[:, :])
                        high_low(st, pt[:, c0 + 1, :], pt[:, c0 + 2, :], rest[:, :])
                    st.end()
                    g.nop().then_inc(S["prep_done"], 1)
                if b.within(1, 1):
                    for n in range(2):
                        pool.dma_start(stage[:, n, :], wpack[0, :, n * CH:(n + 1) * CH]).then_inc(w_in[n], 16)
                if b.within(2, 1 + NCH):
                    n = b.n - 2
                    split_chunk(0, n * CH, n, b.pair - 1, b.parity, moving=True)
                    if b.within(2, NCH - 1):
                        pool.dma_start(stage[:, b.parity, :], wpack[0, :, bass.ds((n + 2) * CH, CH)]) \
                            .then_inc(w_in[b.parity], 16)
                    if b.within(1 + NCH, 1 + NCH):
                        g.nop().then_inc(S["w_ready"], 1)
                pv2 = b.plus(-2)
                if pv2.within(0, B - 1):
                    hold(S["idx_ready"], b.n - 1)
                    for a in range(2):
                        pool.indirect_dma_start(
                            out=zs[:, :], out_offset=bass.IndirectOffsetOnAxis(ap=idx[:, b.parity, a:a + 1], axis=0),
                            in_=z[:, b.parity, :], in_offset=None).then_inc(slots_out[b.parity], 16)
                pv = b.plus(-1)
                if pv.within(0, B - 1):
                    hold(S["t_ready"], b.n)
                    if pv.within(1, B - 1):
                        hold(S["x1_kept"], b.n - 1)
                    xr = xres[:, bass.ds(pv.n, 1), :].rearrange("p o q -> p (o q)")
                    g.tensor_tensor(x1[:, :], xr, tb[:, :], ALU.add).then_inc(S["x1_ready"], 1)
                    hold(S["st2_ready"], b.n)
                    st = Steps(hold, S["z_steps"], pv.n, ENGINE_STEPS["z"])
                    if pv.within(2, B - 1):
                        hold(S["zt_ps"], b.n - 2)
                        hold(slots_out[pv.parity], pv.pair * 32)
                    st.step(g.tensor_scalar(zsc[:, 0:1], mv2[:, 1:2], EPS, 1.0, ALU.add, ALU.mult))
                    st.step(g.tensor_tensor(zsc[:, 1:2], zsc[:, 0:1], mhalf[:, :], ALU.pow))
                    st.step(g.tensor_scalar(zsc[:, 2:3], mv2[:, 0:1], -1.0, 0.0, ALU.mult, ALU.add))
                    st.step(g.tensor_scalar(z[:, pv.parity, :], x1[:, :], zsc[:, 2:3], zsc[:, 1:2], ALU.add, ALU.mult))
                    st.end()
                    g.nop().then_inc(S["z_ready"], 1)

            slots(pool, slot)

            def expert(e, e_par, n0):
                for ch in range(2):
                    pool.dma_start(stage[:, ch, :], wpack[bass.ds(e, 1), :, ch * CH:(ch + 1) * CH].rearrange(
                        "o p c -> p (o c)")).then_inc(w_in[ch], 16)
                for ch in range(NCH):
                    split_chunk(e_par, ch * CH, n0 + ch, (n0 + ch - ch % 2) // 2 if isinstance(n0, int)
                                else e * (NCH // 2) + ch // 2, ch % 2)
                    if ch + 2 < NCH:
                        pool.dma_start(stage[:, ch % 2, :], wpack[bass.ds(e, 1), :, (ch + 2) * CH:(ch + 3) * CH]
                                       .rearrange("o p c -> p (o c)")).then_inc(w_in[ch % 2], 16)
                g.nop().then_inc(S["w_ready"], 1)

            hold(S["attn_done"], 1)
            expert(1, 1, NCH)
            hold(S["tab_ready"], 1)
            with pool.Fori(1, E // 2) as i:
                for par in range(2):
                    e = i * 2 + par
                    last = pool.value_load(etab[0:1, 1, bass.ds(e - 2, 1)], min_val=1, max_val=T + 1)
                    hold(S["tiles_done"], last)
                    expert(e, par, e * NCH)

            hold(y_out[0], 16 * ((T + 1) // 2))
            hold(y_out[1], 16 * (T // 2))

            def gather(b, r):
                for a in range(2):
                    pool.indirect_dma_start(
                        out=gb[:, r, a, :], out_offset=None, in_=ys[:, :],
                        in_offset=bass.IndirectOffsetOnAxis(ap=fidx[:, b, a:a + 1], axis=0)) \
                        .then_inc(g_in[r], 16)

            for b in range(B):
                if b >= 4:
                    hold(S["comb_done"], b - 3)
                gather(b, b % 4)

        @block.scalar
        def _(act):
            s = nc.scalar
            act.wait_ge(S["len_in"], 16)
            s.activation(len_f[:, :], len_i[:, :], ACT.Copy).then_inc(S["ln_ready"], 1)
            act.wait_ge(S["ln_ready"], 1)
            s.activation(sb_col[:, :], len_f[:, :], ACT.Ln).then_inc(S["ln_ready"], 1)

            def slot(b):
                nb, pv, pv2 = b.plus(1), b.plus(-1), b.plus(-2)
                full, behind = b.within(0, B - 1), pv.within(0, B - 1)

                def exps(w, us_):
                    if not full:
                        return
                    for u in us_:
                        j, kk = u // 2, u % 2
                        if u == 0 and (w >= 2 or b.within(1, B - 1)):
                            act.wait_ge(S["pv_done"], b.n * 4 + (w - 1))
                        act.wait_ge(S["scores_ready"], b.n * 32 + (8 * w + u + 1))
                        s.activation(probs[:, w % 2, j, kk, :], sc[u % 2][:, :], ACT.Exp) \
                            .then_inc(S["exp_done"], 1)

                def take_out(bb, gr):
                    act.wait_ge(S["pv_done"], bb.n * 4 + 2 * gr + 2)
                    if bb.within(1, B - 1):
                        act.wait_ge(S["u_ready"], bb.n)
                        act.wait_ge(S["sums_out"], bb.n * 32)
                    s.activation(og[:, gr, :], ob[:, :], ACT.Copy).then_inc(S["og_ready"], 1)

                exps(0, range(0, 1))
                if pv2.within(0, B - 1):
                    act.wait_ge(S["zt_ps"], b.n - 1)
                    if b.within(3, B + 1):
                        act.wait_ge(S["gate_ready"], b.n - 2)
                    s.activation(zt[:, :, :].rearrange("p k t -> p (k t)"), misc[:, :], ACT.Copy) \
                        .then_inc(S["zt_ready"], 1)
                exps(0, range(1, 8))
                if pv.within(0, B - 1):
                    take_out(pv, 1)
                if nb.within(0, B - 1):
                    act.wait_ge(S["vt_ps"], b.n + 2)
                    s.activation(vt[:, nb.parity, :, :, 0:DH], misc[:, :].rearrange("p (k h d) -> p k h d", k=4, h=H),
                                 ACT.Copy).then_inc(S["vt_ready"], 1)
                exps(1, range(0, 4))
                if pv.within(0, B - 1):
                    act.wait_ge(S["u_ready"], b.n)
                    if pv.within(1, B - 1):
                        act.wait_ge(S["t_ready"], b.n - 1)
                    s.activation(us[:, :], misc[:, :], ACT.Copy).then_inc(S["us_ready"], 1)
                exps(1, range(4, 8))
                exps(2, range(8))
                if full:
                    take_out(b, 0)
                exps(3, range(0, 7))
                if behind:
                    act.wait_ge(S["x1_ready"], b.n)
                    s.activation(xres[:, bass.ds(pv.n, 1), :].rearrange("p o q -> p (o q)"), x1[:, :], ACT.Copy) \
                        .then_inc(S["x1_kept"], 1)
                exps(3, range(7, 8))

            slots(act, slot)

            act.wait_ge(S["routed"], 1)
            s.activation(gexp[:, :], gexp[:, :], ACT.Exp).then_inc(S["gexp_ready"], 1)

            def x_high(t, par):
                act.wait_ge(S["xt_ps"], t + 1)
                s.activation(xT[:, par, 0], misc[:, :].rearrange("p (k t) -> p k t", k=KD), ACT.Copy) \
                    .then_inc(S["xt_hi"], 1)

            def tile(t, par, first=False, last=False):
                if not first:
                    act.wait_ge(S["h_ready"], t * 2)
                for n in range(2):
                    act.wait_ge(S["up_ready"], t * 2 + n + 1)
                    s.activation(act_g[:, n * 512:(n + 1) * 512], up[n][0], ACT.Silu).then_inc(S["silu_done"], 1)
                if not last:
                    x_high(t + 1, 1 - par)
                act.wait_ge(S["ht_ps"], t + 1)
                for n in range(2):
                    s.activation(hT[:, par, 0, 4 * n:4 * n + 4, :], hTp[n][:, :].rearrange("p (k t) -> p k t", k=4),
                                 ACT.Copy).then_inc(S["ht_hi"], 1)

            x_high(0, 0)
            tile(0, 0, first=True)
            with act.Fori(0, (T - 3) // 2) as i:
                tile(i * 2 + 1, 1)
                tile(i * 2 + 2, 0)
            tile(T - 2, 1)
            tile(T - 1, 0, last=True)

        @block.vector
        def _(dve):
            v = nc.vector
            v.memset(ks[96:128], 0.0).then_inc(S["rows_set"], 1)
            v.memset(qs[96:128], 0.0).then_inc(S["rows_set"], 1)
            dve.wait_ge(S["rows_set"], 2)
            v.memset(ks[96:98], 1.0).then_inc(S["rows_set"], 1)
            dve.wait_ge(S["ln_ready"], 2)
            v.tensor_scalar(sb_col[:, :], sb_col[:, :], SCALE, None, ALU.mult).then_inc(S["sb_ready"], 1)
            dve.wait_ge(S["consts"], N_CONST)

            st = Steps(dve.wait_ge, S["table_chain"], 0, 5)
            dve.wait_ge(S["numbered"], 1)
            st.step(v.tensor_copy(tio[:, 0, :], tio_i[:, :]))
            st.step(v.tensor_copy(numbers[:, :], tio_i[:, 0:E]))
            st.step(v.tensor_scalar(first_rows[:, :], numbers[:, :], float(REG), None, ALU.mult))
            st.step(v.tensor_scalar(tio[:, 1, :], tio[:, 0, :], float(P), None, ALU.mult))
            st.step(v.tensor_tensor(upto[:, :, :], numbers[:, :].unsqueeze(2).to_broadcast([P, E, E]),
                                    numbers[:, :].unsqueeze(1).to_broadcast([P, E, E]), ALU.is_ge))
            st.end()
            v.memset(mask_sum[:, :], 0.0).then_inc(S["rows_set"], 1)
            dve.wait_ge(S["rows_set"], 4)

            def slot(b):
                nb, pv, pv2, ahead2 = b.plus(1), b.plus(-1), b.plus(-2), b.plus(2)

                def maxima(ks_):
                    for i in ks_:
                        k = (i + LEAD) % 16
                        bb = nb if i + LEAD < 16 else ahead2
                        if not bb.within(0, B - 1):
                            continue
                        if k == 0 and bb.within(2, B - 1):
                            dve.wait_ge(S["mt_ready"], bb.n - 1)
                        dve.wait_ge(S["p1_ready"], bb.n * 16 + (k + 1))
                        v.tensor_reduce(nm[:, bb.parity, 2 * k:2 * k + 2],
                                        p1[k % 2][:, :].rearrange("p (c k) -> p c k", c=2), AX_X, ALU.max,
                                        negate=True).then_inc(S["p1_used"], 1)

                routes = pv2.within(0, B - 1)
                maxima(range(0, 2))
                if routes:
                    a_steps = Steps(dve.wait_ge, S["route_a_steps"], pv2.n, ENGINE_STEPS["route_a"])
                    dve.wait_ge(S["gate_ready"], b.n - 1)
                    two = experts2[:, bass.ds(pv2.n, 1), :].rearrange("p o a -> p (o a)")
                    v.nop().then_inc(S["dve_held"], 1)
                    a_steps.step(v.max(sorted8[:, :], misc[:, 0:E]))
                    v.nop().then_inc(S["dve_held"], 1)
                    a_steps.step(v.max_index(order8[:, :], sorted8[:, :], misc[:, 0:E]))
                    v.nop().then_inc(S["gate_used"], 1)
                maxima(range(2, 3))
                if routes:
                    a_steps.step(v.tensor_copy(scores2[:, bass.ds(pv2.n, 1), :].rearrange("p o a -> p (o a)"),
                                               sorted8[:, 0:2]))
                    a_steps.step(v.tensor_copy(two, order8[:, 0:2]))
                    a_steps.step(v.tensor_tensor(masks[:, :, :], numbers[:, :].unsqueeze(1).to_broadcast([P, 2, E]),
                                                 two.unsqueeze(2).to_broadcast([P, 2, E]), ALU.is_equal))
                    a_steps.step(v.tensor_tensor(maskb[:, :], masks[:, 0, :], masks[:, 1, :], ALU.add))
                    a_steps.end()
                    v.nop().then_inc(S["mask_ready"], 1)
                maxima(range(3, 7))
                if pv.within(0, B - 1):
                    dve.wait_ge(S["den_in"], b.n * 16)
                    if pv.within(1, B - 1):
                        dve.wait_ge(S["rec_out"], b.n * 16 - 16)
                    v.reciprocal(rden[:, :], den[:, :]).then_inc(S["rec_ready"], 1)
                if routes:
                    b_steps = Steps(dve.wait_ge, S["route_b_steps"], pv2.n, ENGINE_STEPS["route_b"])
                    dve.wait_ge(S["rank_ready"], b.n - 1)
                    b_steps.step(v.tensor_tensor(place[:, 2, :], misc[:, 0:E], first_rows[:, :], ALU.add))
                    v.nop().then_inc(S["rank_used"], 1)
                    b_steps.step(v.tensor_tensor(mask_sum[:, :], mask_sum[:, :], maskb[:, :], ALU.add))
                    b_steps.step(v.tensor_tensor(place[:, 0:2, :], masks[:, :, :],
                                                 place[:, 2, :].unsqueeze(1).to_broadcast([P, 2, E]), ALU.mult))
                if routes:
                    row = rows[:, bass.ds(pv2.n, 1), :].rearrange("p o a -> p (o a)")
                    b_steps.step(v.tensor_reduce(row, place[:, 0:2, :], AX_X, ALU.add))
                    if b.within(4, B + 1):
                        dve.wait_ge(slots_out[pv2.parity], pv2.pair * 32)
                    v.nop().then_inc(S["dve_held"], 1)
                    b_steps.step(v.tensor_copy(idx[:, b.parity, :], row))
                    b_steps.end()
                    v.nop().then_inc(S["idx_ready"], 1)
                maxima(range(7, 10))
                lb = b.plus(3)
                if lb.within(0, B - 1):
                    dve.wait_ge(loads[lb.parity], lb.pair * 32 + 32)
                    if lb.within(2, B - 1):
                        dve.wait_ge(S["prep_done"], b.n + 2)
                    if lb.within(1, B - 1):
                        dve.wait_ge(S["st1_ready"], b.n + 3)
                    v.bn_stats(st1[:, :], xres[:, bass.ds(lb.n, 1), :].rearrange("p o q -> p (o q)")) \
                        .then_inc(S["st1_steps"], 1)
                    dve.wait_ge(S["st1_steps"], b.n + 4)
                    v.nop().then_inc(S["dve_held"], 1)
                    v.bn_aggr(mv1[:, lb.parity, :], st1[:, :]).then_inc(S["st1_ready"], 1)
                maxima(range(10, 11))
                if nb.within(0, B - 1):
                    dve.wait_ge(S["mt_ready"], b.n + 2)
                    if nb.within(1, B - 1):
                        dve.wait_ge(S["m_out"], b.n * 16 + 16)
                    v.tensor_copy(mrow[:, 0, :], misc[0:32, 0:P]).then_inc(S["m_steps"], 1)
                    dve.wait_ge(S["m_steps"], b.n + 2)
                    v.tensor_tensor(mrow[:, 1, :], misc[0:32, 0:P], mrow[:, 0, :], ALU.subtract) \
                        .then_inc(S["m_ready"], 1)
                maxima(range(11, 12))
                if pv.within(0, B - 1):
                    dve.wait_ge(S["r_ready"], b.n)
                    dve.wait_ge(S["us_ready"], b.n)
                    if pv.within(1, B - 1):
                        dve.wait_ge(S["x1_ready"], b.n - 1)
                    v.tensor_tensor(tb[:, :], misc[:, :], us[:, :], ALU.mult).then_inc(S["t_ready"], 1)
                maxima(range(12, 14))
                if pv.within(0, B - 1):
                    dve.wait_ge(S["x1_ready"], b.n)
                    if pv.within(1, B - 1):
                        dve.wait_ge(S["st2_ready"], b.n - 1)
                    v.bn_stats(st2[:, :], x1[:, :]) \
                        .then_inc(S["st2_steps"], 1)
                    dve.wait_ge(S["st2_steps"], b.n)
                    if pv.within(1, B - 1):
                        dve.wait_ge(S["z_ready"], b.n - 1)
                    v.nop().then_inc(S["dve_held"], 1)
                    v.bn_aggr(mv2[:, :], st2[:, :]).then_inc(S["st2_ready"], 1)
                maxima(range(14, 16))

            slots(dve, slot)

            st = Steps(dve.wait_ge, S["table_chain"], 1, 5)
            link = st.step
            dve.wait_ge(S["pv_done"], 4 * B)
            link(v.tensor_tensor(gexp[:, :].unsqueeze(2), scores2[:, :, 1:2], scores2[:, :, 0:1], ALU.subtract))
            v.nop().then_inc(S["routed"], 1)
            link(v.memset(cv[:, :], 0.0))
            link(v.tensor_tensor(c3, numbers[:, :].unsqueeze(1).to_broadcast([P, 2 * B, E]),
                                 experts2[:, :, :].rearrange("p b a -> p (b a)").unsqueeze(2).to_broadcast([P, 2 * B, E]), ALU.is_equal))
            dve.wait_ge(S["cnt_ready"], 1)
            cnt = misc[:, 0:E]
            link(v.tensor_tensor(zero_rows, cnt, first_rows[:, :], ALU.add))
            link(v.tensor_copy(etab[:, 0, :], zero_rows))
            v.nop().then_inc(S["zero_ready"], 1)
            link(v.tensor_tensor(k3, cnt.unsqueeze(2).to_broadcast([P, E, B]),
                                 tio[:, 1, 0:B].unsqueeze(1).to_broadcast([P, E, B]), ALU.is_gt))
            link(v.tensor_reduce(tiles, k3, AX_X, ALU.add))
            link(v.tensor_tensor(upto[:, :, :], upto[:, :, :], tiles.unsqueeze(1).to_broadcast([P, E, E]), ALU.mult))
            link(v.tensor_reduce(cum, upto[:, :, :], AX_X, ALU.add))
            link(v.tensor_scalar(etab[:, 1, :], cum, 1.0, None, ALU.add))
            link(v.tensor_tensor(t3, tio[:, 0, :].unsqueeze(2).to_broadcast([P, T, E - 1]),
                                 cum[:, 0:E - 1].unsqueeze(1).to_broadcast([P, T, E - 1]), ALU.is_ge))
            link(v.tensor_reduce(expt, t3, AX_X, ALU.add))
            link(v.tensor_scalar(tab[:, 2, :], expt, 1.0, None, ALU.add))
            link(v.tensor_copy(tab[:, 1, :], expt))
            link(v.tensor_scalar(tab[:, 1, :], tab[:, 1, :], 1, None, ALU.bitwise_and))
            link(v.tensor_scalar(delta, tiles, -float(P), float(REG), ALU.mult, ALU.add))
            link(v.tensor_tensor(t3, t3, delta[:, 0:E - 1].unsqueeze(1).to_broadcast([P, T, E - 1]), ALU.mult))
            link(v.tensor_reduce(row_t, t3, AX_X, ALU.add))
            link(v.tensor_tensor(row_t, row_t, tio[:, 1, :], ALU.add))
            link(v.tensor_scalar(tab[:, 0, :], row_t, zero_rows[:, E - 1:E], None, ALU.min))
            v.nop().then_inc(S["tab_ready"], 1)
            link(v.tensor_tensor(tbase, cum, tiles, ALU.subtract))
            link(v.scalar_tensor_tensor(base, tbase, -float(P), first_rows[:, :], ALU.mult, ALU.add))
            link(v.tensor_tensor(c3, c3, base.unsqueeze(1).to_broadcast([P, 2 * B, E]), ALU.mult))
            link(v.tensor_reduce(at_base, c3, AX_X, ALU.add))
            link(v.tensor_tensor(fidx[:, :, :], rows[:, :, :], at_base.rearrange("p (b a) -> p b a", a=2), ALU.subtract))
            dve.wait_ge(S["gexp_ready"], 1)
            link(v.tensor_scalar(gate[:, 1, :], gexp[:, :], 1.0, None, ALU.add))
            link(v.reciprocal(gate[:, 0, :], gate[:, 1, :]))
            link(v.tensor_tensor(gate[:, 1, :], gexp[:, :], gate[:, 0, :], ALU.mult))

            def x_low(t, par):
                dve.wait_ge(S["xt_hi"], t + 1)
                v.tensor_tensor(xT[:, par, 1], misc[:, :].rearrange("p (k t) -> p k t", k=KD), xT[:, par, 0],
                                ALU.subtract).then_inc(S["xt_lo"], 1)

            def take_y(t, par, early=False):
                dve.wait_ge(S["tiles_done"], t + 2)
                if not early:
                    dve.wait_ge(y_out[par], (t - par) * 8)
                v.tensor_copy(yb[:, par, :], ob[:, :]).then_inc(S["yb_ready"], 1)

            def tile(t, par, first=False, last=False, early=False):
                if not first:
                    dve.wait_ge(S["ht_ps"], t)
                for n in range(2):
                    dve.wait_ge(S["silu_done"], t * 2 + n + 1)
                    v.tensor_tensor(hbuf[:, n * 512:(n + 1) * 512], up[n][1], act_g[:, n * 512:(n + 1) * 512],
                                    ALU.mult).then_inc(S["h_ready"], 1)
                if not last:
                    x_low(t + 1, 1 - par)
                if not first:
                    take_y(t - 1, 1 - par, early)
                for n in range(2):
                    dve.wait_ge(S["ht_hi"], t * 2 + n + 1)
                    v.tensor_tensor(hT[:, par, 1, 4 * n:4 * n + 4, :], hTp[n][:, :].rearrange("p (k t) -> p k t", k=4),
                                    hT[:, par, 0, 4 * n:4 * n + 4, :], ALU.subtract).then_inc(S["ht_lo"], 1)

            x_low(0, 0)
            tile(0, 0, first=True)
            tile(1, 1, early=True)
            tile(2, 0, early=True)
            with dve.Fori(1, (T - 3) // 2) as i:
                tile(i * 2 + 1, 1)
                tile(i * 2 + 2, 0)
            tile(T - 2, 1)
            tile(T - 1, 0, last=True)
            take_y(T - 1, 0)

            v.nop().then_inc(S["comb_steps"], 1)
            with dve.Fori(0, B // 4) as i:
                for r in range(4):
                    b = i * 4 + r
                    dve.wait_ge(g_in[r], i * 32 + 32)
                    xr = xres[:, bass.ds(b, 1), :].rearrange("p o q -> p (o q)")
                    v.scalar_tensor_tensor(xr, gb[:, r, 0, :], gate[:, 0, bass.ds(b, 1)], xr, ALU.mult, ALU.add) \
                        .then_inc(S["comb_steps"], 1)
                    dve.wait_ge(S["comb_steps"], b + 2)
                    v.scalar_tensor_tensor(xr, gb[:, r, 1, :], gate[:, 1, bass.ds(b, 1)], xr, ALU.mult, ALU.add) \
                        .then_inc(S["comb_done"], 1)

        @block.tensor
        def _(pe):
            m = nc.tensor
            pe.wait_ge(S["consts"], N_CONST)
            pe.wait_ge(S["rows_set"], 3)
            pe.wait_ge(S["gate_in"], 16)

            def slot(b):
                nb, pv, pv2 = b.plus(1), b.plus(-1), b.plus(-2)
                full, ahead = b.within(0, B - 1), nb.within(0, B - 1)
                behind = pv.within(0, B - 1)
                def rows_unit(i):
                    k = (i + LEAD) % 16
                    bb = nb if i + LEAD < 16 else b.plus(2)
                    if not bb.within(0, B - 1):
                        return
                    hh, qh = k // 2, k % 2
                    if k % 8 == 0:
                        pe.wait_ge(st_in[bb.parity][k // 8], bb.pair * 32 + 32)
                    if k >= 2 or bb.within(1, B - 1):
                        pe.wait_ge(S["p1_used"], bb.n * 16 + (k - 1))
                    for c in range(2):
                        q0 = (2 * qh + c) * P
                        ins = m.matmul(p1[k % 2][:, c * 512:(c + 1) * 512], qs[0:KROWS, bb.parity, hh, q0:q0 + P],
                                       ks[0:KROWS, bb.parity, hh, :], start=True, stop=True)
                    ins.then_inc(S["p1_ready"], 1)

                def score(w, u):
                    j, kk = u // 2, u % 2
                    h, kc = 4 * (w // 2) + j, 2 * (w % 2) + kk
                    if w == 0 and u == 0:
                        pe.wait_ge(S["m_in"], b.n * 16 + 16)
                    if w or u >= 2 or b.within(1, B - 1):
                        pe.wait_ge(S["exp_done"], b.n * 32 + (8 * w + u - 1))
                    m.matmul(sc[u % 2][:, :], ks[:, b.parity, h, kc * P:(kc + 1) * P], qs[:, b.parity, h, :],
                             start=True, stop=True).then_inc(S["scores_ready"], 1)

                def values(bb, w, kk):
                    if kk == 0:
                        pe.wait_ge(S["exp_done"], bb.n * 32 + 8 * (w + 1))
                        if w == 0:
                            pe.wait_ge(S["vt_ready"], bb.n + 1)
                        if w == 2 or (w == 0 and bb.within(1, B - 1)):
                            pe.wait_ge(S["og_ready"], bb.n * 2 + w // 2)
                    kc = 2 * (w % 2) + kk
                    for j in range(4):
                        ins = m.matmul(ob[32 * j:32 * j + 32, :], vt[:, bb.parity, kc, 4 * (w // 2) + j, :],
                                       probs[:, w % 2, j, kk, :], start=(kc == 0), stop=(kc == 3))
                    if kk == 1:
                        ins.then_inc(S["pv_done"], 1)

                reader = (S["zt_ready"], b.n - 1) if pv2.within(0, B - 1) else \
                    (S["m_ready"], b.n + 1) if full else None

                for w in range(4):
                    for u in range(8):
                        if u % 2 == 0:
                            rows_unit(4 * w + u // 2)
                        if full:
                            score(w, u)
                        if (w, u) == (0, 3) and pv2.within(0, B - 1):
                            pe.wait_ge(*reader)
                            for k in range(KD):
                                ins = m.matmul(misc[:, 0:E], zt[:, k, :], gw[:, k, :], start=(k == 0),
                                               stop=(k == KD - 1))
                            ins.then_inc(S["gate_ready"], 1)
                            reader = (S["gate_used"], b.n - 1)
                        if u in (3, 6):
                            kk = 0 if u == 3 else 1
                            if w == 0 and behind:
                                values(pv, 3, kk)
                            if w > 0 and full:
                                values(b, w - 1, kk)
                        if (w, u) == (0, 7) and ahead:
                            pe.wait_ge(S["cv_in"], b.n * 16 + 32)
                            if reader:
                                pe.wait_ge(*reader)
                            for kc in range(4):
                                ins = m.transpose(misc[:, kc * P:(kc + 1) * P], cv[:, kc * P:(kc + 1) * P], ident[:, :])
                            ins.then_inc(S["vt_ps"], 1)
                            reader = (S["vt_ready"], b.n + 2)
                        if (w, u) == (1, 2) and behind:
                            if reader:
                                pe.wait_ge(*reader)
                            pe.wait_ge(S["og_ready"], b.n * 2)
                            for gr in range(2):
                                ins = m.matmul(misc[:, :], selu[:, gr, :], og[:, gr, :], start=(gr == 0), stop=(gr == 1))
                            ins.then_inc(S["u_ready"], 1)
                            reader = (S["us_ready"], b.n)
                        if (w, u) == (1, 4) and pv2.within(0, B - 1):
                            pe.wait_ge(*reader)
                            pe.wait_ge(S["mask_ready"], b.n - 1)
                            m.matmul(misc[:, 0:E], ltri[:, :], maskb[:, :], start=True, stop=False)
                            m.matmul(misc[:, 0:E], onesb[:, :], mask_sum[:, :], start=False, stop=True) \
                                .then_inc(S["rank_ready"], 1)
                            reader = (S["rank_used"], b.n - 1)
                        if (w, u) == (2, 6) and ahead:
                            pe.wait_ge(S["p1_used"], b.n * 16 + 32)
                            if reader:
                                pe.wait_ge(*reader)
                            m.transpose(misc[:, 0:P], nm[:, nb.parity, :], ident[:, :]).then_inc(S["mt_ready"], 1)
                            reader = (S["m_ready"], b.n + 2)
                        if (w, u) == (2, 7) and behind:
                            pe.wait_ge(S["rec_in"], b.n * 16)
                            pe.wait_ge(*reader)
                            m.matmul(misc[:, :], selb[:, :], r8[:, :], start=True, stop=True).then_inc(S["r_ready"], 1)
                            reader = (S["t_ready"], b.n)
                        if (w, u) == (3, 6) and behind:
                            pe.wait_ge(S["z_ready"], b.n)
                            pe.wait_ge(*reader)
                            for k in range(KD):
                                ins = m.transpose(misc[:, k * P:(k + 1) * P], z[:, pv.parity, k * P:(k + 1) * P],
                                                  ident[:, :])
                            ins.then_inc(S["zt_ps"], 1)

            slots(pe, slot)
            pe.wait_ge(S["og_ready"], 2 * B)
            m.nop().then_inc(S["attn_done"], 1)
            pe.wait_ge(S["rank_used"], B)
            pe.wait_ge(S["route_b_steps"], ENGINE_STEPS["route_b"] * B)
            m.matmul(misc[:, 0:E], onesb[:, :], mask_sum[:, :], start=True, stop=True).then_inc(S["cnt_ready"], 1)

            pe.wait_ge(S["tab_ready"], 1)
            m.nop().then_inc(S["tiles_done"], 1)

            def x_tile(t, par, first=False):
                pe.wait_ge(xrow_in[par], (t - par) * 8 + 16)
                if not first:
                    pe.wait_ge(S["xt_lo"], t)
                for k in range(KD):
                    ins = m.transpose(misc[:, k * P:(k + 1) * P], xrow[:, par, k * P:(k + 1) * P], ident[:, :])
                ins.then_inc(S["xt_ps"], 1)

            def split_products(bank, stat, w_off, n_chunks, stride, col):
                for k in range(n_chunks):
                    for n, (s_part, w_part) in enumerate(((0, 0), (0, 1), (1, 0))):
                        at_w = w_off + (w_part * WLEN + col + k * stride)
                        ins = m.matmul(bank, stat[:, s_part, k, :], W[:, bass.ds(at_w, 512)],
                                       start=(k == 0 and n == 0), stop=(k == n_chunks - 1 and n == 2))
                return ins

            def half_of(t):
                e = pe.value_load(tab[0:1, 1, bass.ds(t, 1)], min_val=0, max_val=1)
                return e * half

            def up_tile(t, par, first=False):
                ready = pe.value_load(tab[0:1, 2, bass.ds(t, 1)], min_val=1, max_val=E)
                off = half_of(t)
                pe.wait_ge(S["w_ready"], ready)
                pe.wait_ge(S["xt_lo"], t + 1)
                for n in range(2):
                    if not first:
                        pe.wait_ge(S["h_ready"], t * 2 - 1 + n)
                    for wn in range(2):
                        ins = split_products(up[n][wn], xT[:, par], off, KD, I, wn * KD * I + n * 512)
                    ins.then_inc(S["up_ready"], 1)

            def down_tile(t, par, first=False):
                off = half_of(t)
                pe.wait_ge(S["ht_lo"], t * 2 + 2)
                if not first:
                    pe.wait_ge(S["yb_ready"], t)
                ins = split_products(ob[:, :], hT[:, par], off, KI, D, 2 * KD * I)
                ins.then_inc(S["tiles_done"], 1)

            def h_tile(t, par, first=False):
                pe.wait_ge(S["h_ready"], t * 2 + 2)
                if not first:
                    pe.wait_ge(S["ht_lo"], t * 2)
                for k in range(KI):
                    ins = m.transpose(hTp[k // 4][:, (k % 4) * P:(k % 4 + 1) * P], hbuf[:, k * P:(k + 1) * P], ident[:, :])
                ins.then_inc(S["ht_ps"], 1)

            def tile(t, par, last=False, second=False):
                up_tile(t, par)
                if not last:
                    x_tile(t + 1, 1 - par)
                down_tile(t - 1, 1 - par, first=second)
                h_tile(t, par)

            x_tile(0, 0, first=True)
            up_tile(0, 0, first=True)
            x_tile(1, 1)
            h_tile(0, 0, first=True)
            tile(1, 1, second=True)
            tile(2, 0)
            with pe.Fori(1, (T - 3) // 2) as i:
                tile(i * 2 + 1, 1)
                tile(i * 2 + 2, 0)
            tile(T - 2, 1)
            tile(T - 1, 0, last=True)
            down_tile(T - 1, 0)


def kernel(x, ctx_2048, itok_B_779_1933, L0_ffn_gate_w, L0_ffn_w1, L0_ffn_w2, L0_ffn_w3):
    import concourse.bacc as _bacc
    from concourse.bass_utils import run_bass_kernel_spmd as _run

    def chunked(w):
        w = np.asarray(w)
        e, o, i = w.shape
        return w.transpose(0, 2, 1).reshape(e, i // P, P, o).transpose(0, 2, 1, 3).reshape(e, P, i // P * o)

    arrays = {
        "x_dram": np.ascontiguousarray(x),
        "ctx_dram": np.ascontiguousarray(ctx_2048),
        "lengths_dram": np.ascontiguousarray(itok_B_779_1933),
        "wpack_dram": np.ascontiguousarray(np.concatenate(
            [chunked(L0_ffn_w1), chunked(L0_ffn_w3), chunked(L0_ffn_w2)], axis=2)),
        "gate_dram": np.ascontiguousarray(np.asarray(L0_ffn_gate_w).T),
    }
    nc = _bacc.Bacc("TRN2", target_bir_lowering=False, num_devices=1)
    args = [nc.dram_tensor(n, a.shape, mybir.dt.from_np(a.dtype), kind="ExternalInput").ap() for n, a in arrays.items()]
    out = nc.dram_tensor("out_dram", arrays["x_dram"].shape, F32, kind="ExternalOutput").ap()
    build(nc, *args, out)
    r = _run(nc, [arrays], core_ids=[0])
    return r.results[0]["out_dram"]
```

```python
from contextlib import ExitStack

import numpy as np

import concourse.bass as bass
from concourse import mybir

ALU = mybir.AluOpType
ACT = mybir.ActivationFunctionType
F32 = mybir.dt.float32
BF16 = mybir.dt.bfloat16
I32 = mybir.dt.int32
U32 = mybir.dt.uint32
AX_X = mybir.AxisListType.X

P = 128
LOOP_FIRST, LOOP_LAST = 2, 6
LEAD = 4
ENGINE_STEPS = {"prep": 10, "keys": 4, "z": 4, "route_a": 6, "route_b": 5}


class Batch:

    def __init__(self, pair, parity, low, high):
        self.pair, self.parity = pair, parity
        self.low, self.high = low, high

    @property
    def n(self):
        return self.pair * 2 + self.parity

    def plus(self, k):
        p = self.parity + k
        return Batch(self.pair + p // 2, p % 2, self.low + k, self.high + k)

    def within(self, first, last):
        inside = first <= self.low and self.high <= last
        assert inside or self.high < first or self.low > last
        return inside


class Steps:

    def __init__(self, wait, sem, index, each):
        self.wait, self.sem, self.index, self.each, self.done = wait, sem, index, each, 0

    def step(self, instruction):
        self.done += 1
        instruction.then_inc(self.sem, 1)
        self.wait(self.sem, self.index * self.each + self.done)

    def end(self):
        assert self.done == self.each, (self.done, self.each)


def build(nc, x, ctx_kv, lengths, wpack, gate_t, out):
    B, HD, L = x.shape
    LK = ctx_kv.shape[2]
    H = 8
    DH = HD // H
    E, _, WLEN = wpack.shape
    D = L
    I = WLEN // (3 * D // P)
    KD, KI = D // P, I // P
    assert WLEN == KD * I * 2 + KI * D and HD == P and L == LK == 512
    SCALE = 1.0 / (64 ** 0.5 * float(np.log(20)))
    EPS = 1e-5
    TOK = B * P
    REG = TOK + P
    T = (2 * TOK + E * (P - 1)) // P
    SURE = 2 * TOK // P
    CH = 1024
    NCH = WLEN // CH
    CH2 = 2 * CH
    NCH2 = WLEN // CH2
    KROWS, MROW = 6 * DH, 6 * DH

    pd = nc.dram_tensor("parts_dram", [B, 2, P, 6, L], BF16, kind="Internal").ap()
    zs = nc.dram_tensor("slots_dram", [E * REG, D], F32, kind="Internal").ap()
    ys = nc.dram_tensor("expert_out_dram", [T * P, D], F32, kind="Internal").ap()
    sums_dram = nc.dram_tensor("sums_dram", [B, H, L], F32, kind="Internal").ap()
    recips_dram = nc.dram_tensor("recips_dram", [B, H, L], F32, kind="Internal").ap()
    maxima_dram = nc.dram_tensor("maxima_dram", [B, 2, H * L], BF16, kind="Internal").ap()

    with ExitStack() as cx:
        def sb(name, shape, dt):
            return cx.enter_context(nc.sbuf_tensor(name, shape, dt))

        def pb(name, shape, dt=F32):
            return cx.enter_context(nc.psum_tensor(name, shape, dt))

        def sem(name):
            return cx.enter_context(nc.semaphore(name))

        xres = sb("xres", [P, B, L], F32)
        W = sb("W", [P, 2 * 2 * WLEN], BF16)
        stage = sb("stage", [P, 2, CH], F32)
        ident = sb("ident", [P, P], F32)
        numbers = sb("numbers", [P, E], F32)
        first_rows = sb("first_rows", [P, E], F32)
        scores2 = sb("scores2", [P, B, 2], F32)
        experts2 = sb("experts2", [P, B, 2], F32)
        rows = sb("rows", [P, B, 2], F32)

        half = 2 * WLEN
        probs = W[:, half:half + 16384].bitcast(F32).rearrange("p (b j k q) -> p b j k q", b=2, j=4, k=2)
        ks = W[:, half + 16384:half + 24576].rearrange("p (b h k) -> p b h k", b=2, h=H)
        U = sb("U", [P, 11264], F32)
        qs = U[:, 0:4096].bitcast(BF16).rearrange("p (b h q) -> p b h q", b=2, h=H)
        parts = U[:, 4096:7168].bitcast(BF16).rearrange("p (b c q) -> p b c q", b=2, c=6)
        vt = U[:, 7168:9216].rearrange("p (b k h c) -> p b k h c", b=2, k=4, h=H)
        cin = U[:, 9216:10240].rearrange("p (b k) -> p b k", b=2)
        og = U[:, 10240:11264].rearrange("p (g q) -> p g q", g=2)
        cv = sb("cv", [P, LK], F32)
        norm = sb("norm", [P, L], F32)
        rest = sb("rest", [P, L], F32)
        us = sb("us", [P, L], F32)
        tb = sb("tb", [P, L], F32)
        x1 = sb("x1", [P, L], F32)
        z = sb("z", [P, 2, D], F32)
        zt = sb("zt", [P, KD, P], F32)
        selu = sb("selu", [P, 2, P], F32)
        selb = sb("selb", [8, P], F32)
        r8 = sb("r8", [8, L], F32)
        den = sb("den", [P, 32], F32)
        rden = sb("rden", [P, 32], F32)
        nm = sb("nm", [P, 2, P], F32)
        mrow = sb("mrow", [32, 2, P], BF16)
        len_i = sb("len_i", [P, B], I32)
        len_f = sb("len_f", [P, B], F32)
        sb_col = sb("sb_col", [P, B], F32)
        st1 = sb("st1", [P, 6], F32)
        mv1 = sb("mv1", [P, 2, 2], F32)
        st2 = sb("st2", [P, 6], F32)
        mv2 = sb("mv2", [P, 2], F32)
        mhalf = sb("mhalf", [P, 1], F32)
        zero = sb("zero", [P, 1], F32)
        psc = sb("psc", [P, 4], F32)
        zsc = sb("zsc", [P, 4], F32)
        gw = sb("gw", [P, KD, E], F32)
        sorted8 = sb("sorted8", [P, E], F32)
        order8 = sb("order8", [P, E], U32)
        masks = sb("masks", [P, 2, E], F32)
        place = sb("place", [P, 3, E], F32)
        maskb = sb("maskb", [P, E], BF16)
        mask_sum = sb("mask_sum", [P, E], BF16)
        ltri = sb("ltri", [P, P], BF16)
        onesb = sb("onesb", [P, P], BF16)
        idx = sb("idx", [P, 2, 2], I32)
        tio_i = sb("tio_i", [P, T + 1], I32)
        tio = sb("tio", [P, 2, T + 1], F32)
        upto = sb("upto", [P, E, E], F32)
        tab = sb("tab", [P, 4, T + 1], I32)
        etab = sb("etab", [P, 2, E], I32)
        fidx = sb("fidx", [P, B, 2], I32)
        gexp = sb("gexp", [P, B], F32)
        gate = sb("gate", [P, 2, B], F32)
        small = U[:, 8192:9216]
        t3 = U[:, 7168:7168 + T * (E - 1)].rearrange("p (t e) -> p t e", e=E - 1)
        c3 = U[:, 7680:7680 + 2 * B * E].rearrange("p (n e) -> p n e", e=E)
        k3 = U[:, 7936:7936 + E * B].rearrange("p (e k) -> p e k", k=B)
        tiles, cum, tbase, base, delta, zero_rows = (small[:, n * E:(n + 1) * E] for n in range(6))
        expt, row_t = small[:, 128:128 + T], small[:, 192:192 + T]
        at_base = small[:, 256:256 + 2 * B]

        xrow = U[:, 0:1024].rearrange("p (b d) -> p b d", b=2)
        xT = U[:, 1024:2048].bitcast(BF16).rearrange("p (b s k t) -> p b s k t", b=2, s=2, k=KD)
        act_g = U[:, 2048:3072]
        hbuf = U[:, 3072:4096]
        hT = U[:, 4096:6144].bitcast(BF16).rearrange("p (b s k t) -> p b s k t", b=2, s=2, k=KI)
        yb = U[:, 6144:7168].rearrange("p (b d) -> p b d", b=2)
        stage2 = U[:, 7168:11264].rearrange("p (b c) -> p b c", b=2)
        gb = U[:, 7168:11264].rearrange("p (b a d) -> p b a d", b=4, a=2)

        sc = [pb(f"scores{i}", [P, 512]) for i in range(2)]
        p1 = [pb(f"rows{i}", [P, 1024]) for i in range(2)]
        ob = pb("heads_out", [P, 512])
        misc = pb("misc", [P, 512])
        up = [[p1[0][:, 0:512], p1[1][:, 0:512]], [p1[0][:, 512:1024], p1[1][:, 512:1024]]]
        hTp = [sc[0], sc[1]]

        names = """setup numbered consts rows_set gate_in len_in ln_ready sb_ready table_chain
            prep_steps keys_steps first_keys z_steps route_a_steps route_b_steps queries_out keys_out
            sums_out rec_out m_out den_in rec_in m_in cv_in p1_ready p1_used scores_ready exp_done pv_done
            og_ready vt_ps vt_ready u_ready us_ready r_ready t_ready x1_ready x1_kept zt_ps zt_ready
            gate_ready gate_used mask_ready rank_ready rank_used idx_ready rec_ready st1_steps
            st2_steps st1_ready st2_ready prep_done z_ready mt_ready m_steps m_ready chunk_steps
            chunk2_steps w_ready tab_ready zero_out tiles_done xt_ps xt_hi xt_lo up_ready silu_done h_ready
            ht_ps ht_hi ht_lo yb_ready pool_held dve_held sp_held gexp_ready comb_steps comb_done out_done
            attn_done routed cnt_ready zero_ready tables_done cv_zero table_prep""".split()
        S = {n: sem(n) for n in names}
        loads = [sem(f"loads{i}") for i in range(2)]
        st_in = [[sem(f"stack{i}{j}") for j in range(2)] for i in range(2)]
        slots_out = [sem(f"slots_out{i}") for i in range(2)]
        w_in = [sem(f"w_in{i}") for i in range(2)]
        w2_in = [sem(f"w2_in{i}") for i in range(2)]
        xrow_in = [sem(f"xrow_in{i}") for i in range(2)]
        y_out = [sem(f"y_out{i}") for i in range(2)]
        g_in = [sem(f"g_in{i}") for i in range(4)]

        def slots(engine, body):
            for b in range(-3, 2 * LOOP_FIRST):
                body(Batch(b // 2, b % 2, b, b))
            with engine.Fori(LOOP_FIRST, LOOP_LAST) as i:
                for par in range(2):
                    body(Batch(i, par, 2 * LOOP_FIRST + par, 2 * LOOP_LAST - 2 + par))
            for b in range(2 * LOOP_LAST, B + 2):
                body(Batch(b // 2, b % 2, b, b))

        N_CONST = 10
        block = cx.enter_context(nc.Block())

        @block.sync
        def _(sp):
            sp.dma_start(len_i[:, :], lengths.partition_broadcast(P)).then_inc(S["len_in"], 16)
            sp.dma_start(gw[:, :, :], gate_t.rearrange("(k p) e -> p k e", p=P)).then_inc(S["gate_in"], 16)

            def reload(b, half_h):
                heads = slice(4 * half_h, 4 * half_h + 4)
                for n, stacked in enumerate((qs, ks)):
                    sp.dma_start(stacked[0:KROWS, b.parity, heads, :],
                                 pd[bass.ds(b.n, 1), n, 4 * DH * half_h:4 * DH * (half_h + 1)].rearrange(
                                     "o (h d) c q -> (o d c) h q", h=4)).then_inc(st_in[b.parity][half_h], 16)

            def store_parts(b, n):
                dst = pd[bass.ds(b.n, 1), n].rearrange("o p c q -> (o p) c q")
                src = parts[:, b.parity]
                for first, count, part in ((0, 3, 0), (3, 2, 1), (5, 1, 2)):
                    values = src[:, 0:count, :] if n == 0 else \
                        src[:, 3 + part:4 + part, :].to_broadcast([P, count, L])
                    sp.dma_start(dst[:, first:first + count, :], values).then_inc(S[("queries_out", "keys_out")[n]], 16)

            def slot(b):
                nb = b.plus(1)
                if nb.within(0, B - 1):
                    if b.within(1, B):
                        sp.wait_ge(S["scores_ready"], b.n * 32)
                    reload(nb, 1)
                lb = b.plus(3)
                if lb.within(0, B - 1):
                    if b.within(-1, B):
                        sp.wait_ge(S["keys_steps"], (b.n + 2) * ENGINE_STEPS["keys"])
                    sp.dma_start(xres[:, bass.ds(lb.n, 1), :], x[bass.ds(lb.n, 1)].rearrange("o p q -> p o q")) \
                        .then_inc(loads[lb.parity], 16)
                    sp.dma_start(cin[:, lb.parity, :], ctx_kv[bass.ds(lb.n, 1)].rearrange("o p q -> p (o q)")) \
                        .then_inc(loads[lb.parity], 16)
                pv, pbt = b.plus(-1), b.plus(2)
                behind, ahead2 = pv.within(0, B - 1), pbt.within(0, B - 1)
                if ahead2:
                    sp.wait_ge(S["keys_steps"], (b.n + 3) * ENGINE_STEPS["keys"])
                    store_parts(pbt, 1)
                if behind:
                    sp.wait_ge(S["og_ready"], b.n * 2)
                    for g in range(2):
                        sp.dma_start(sums_dram[bass.ds(pv.n, 1), 4 * g:4 * g + 4].rearrange("o h q -> (o h) q"),
                                     og[16:113:32, g, :]).then_inc(S["sums_out"], 16)
                    sp.wait_ge(S["sums_out"], b.n * 32)
                    sp.dma_start(den[:, :], sums_dram[bass.ds(pv.n, 1)].rearrange("o h (p f) -> (o h p) f", f=32)) \
                        .then_inc(S["den_in"], 16)
                if ahead2:
                    sp.wait_ge(S["prep_done"], b.n + 3)
                    sp.nop().then_inc(S["sp_held"], 1)
                    store_parts(pbt, 0)
                    sp.wait_ge(S["keys_out"], b.n * 48 + 144)
                    sp.nop().then_inc(S["sp_held"], 1)
                    sp.wait_ge(S["queries_out"], b.n * 48 + 144)
                    sp.nop().then_inc(S["sp_held"], 1)
                    if b.within(0, B - 1):
                        sp.wait_ge(S["scores_ready"], b.n * 32 + 16)
                    reload(pbt, 0)
                if behind:
                    sp.wait_ge(S["rec_ready"], b.n)
                    sp.dma_start(recips_dram[bass.ds(pv.n, 1)].rearrange("o h (p f) -> (o h p) f", f=32),
                                 rden[:, :]).then_inc(S["rec_out"], 16)
                if behind:
                    sp.wait_ge(S["rec_out"], b.n * 16)
                    sp.nop().then_inc(S["sp_held"], 1)
                    if b.within(2, B):
                        sp.wait_ge(S["r_ready"], b.n - 1)
                    sp.dma_start(r8[:, :], recips_dram[bass.ds(pv.n, 1)].rearrange("o h q -> (o h) q")) \
                        .then_inc(S["rec_in"], 16)
                if nb.within(0, B - 1):
                    sp.wait_ge(S["m_ready"], b.n + 2)
                    sp.dma_start(maxima_dram[bass.ds(nb.n, 1)].rearrange("o s (c q) -> c (o s) q", q=P),
                                 mrow[:, :, :]).then_inc(S["m_out"], 16)
                    sp.wait_ge(S["m_out"], b.n * 16 + 32)
                    sp.dma_start(qs[MROW:MROW + 2, nb.parity],
                                 maxima_dram[bass.ds(nb.n, 1)].rearrange("o s (h q) -> (o s) h q", h=H)) \
                        .then_inc(S["m_in"], 16)
                if pbt.within(0, B - 1):
                    if nb.within(0, B - 1):
                        sp.wait_ge(S["vt_ps"], b.n + 2)
                    sp.dma_start(cv[:, :], ctx_kv[bass.ds(pbt.n, 1)].rearrange("o p q -> p (o q)")) \
                        .then_inc(S["cv_in"], 16)

            slots(sp, slot)

            sp.wait_ge(S["cv_zero"], 1)
            sp.wait_ge(S["zero_ready"], 1)
            for e in range(0, E, 2):
                r = sp.value_load(etab[0:1, 0, e:e + 1], min_val=0, max_val=E * REG - P)
                sp.dma_start(zs[bass.ds(r, P), :], cv[:, :]).then_inc(S["zero_out"], 16)
            sp.wait_ge(S["zero_out"], 16 * E)
            for i in range(2):
                sp.wait_ge(slots_out[i], 32 * (B // 2))
            sp.wait_ge(S["tab_ready"], 1)

            def load_tile(t, par):
                r = sp.value_load(tab[0:1, 0, bass.ds(t, 1)], min_val=0, max_val=E * REG - P)
                sp.dma_start(xrow[:, par, :], zs[bass.ds(r, P), :]).then_inc(xrow_in[par], 16)

            def store_tile(t, par):
                sp.wait_ge(S["yb_ready"], t + 1)
                sp.dma_start(ys[bass.ds(t * P, P), :], yb[:, par, :]).then_inc(y_out[par], 16)

            load_tile(0, 0)
            load_tile(1, 1)
            with sp.Fori(0, (T - 3) // 2) as i:
                for par in range(2):
                    sp.wait_ge(S["xt_ps"], i * 2 + par + 1)
                    load_tile(i * 2 + par + 2, par)
                    store_tile(i * 2 + par, par)
            sp.wait_ge(S["xt_ps"], T - 2)
            load_tile(T - 1, 0)
            store_tile(T - 3, 0)
            store_tile(T - 2, 1)
            store_tile(T - 1, 0)

            with sp.Fori(0, B) as b:
                sp.wait_ge(S["comb_done"], b + 1)
                sp.dma_start(out[bass.ds(b, 1)].rearrange("o p d -> p o d"), xres[:, bass.ds(b, 1), :]) \
                    .then_inc(S["out_done"], 16)
            sp.wait_ge(S["out_done"], 16 * B)

        @block.gpsimd
        def _(pool):
            g = nc.gpsimd

            def hold(semaphore, value):
                pool.wait_ge(semaphore, value)
                g.nop().then_inc(S["pool_held"], 1)

            c = S["consts"]
            g.memset(mhalf[:, :], -0.5).then_inc(c, 1)
            g.memset(zero[:, :], 0.0).then_inc(c, 1)
            hold(c, 2)

            def constants():
                k = S["setup"]
                g.memset(ident[:, :], 0.0).then_inc(k, 1)
                g.memset(selu[:, :, :], 0.0).then_inc(k, 1)
                g.memset(selb[:, :], 0.0).then_inc(k, 1)
                g.memset(ltri[:, :], 1.0).then_inc(k, 1)
                g.memset(vt, 0.0).then_inc(k, 1)
                hold(k, 5)
                g.affine_select(out=ident[:, :], in_=ident[:, :], compare_op=ALU.not_equal, fill=1.0, base=0,
                                pattern=[[-1, P]], channel_multiplier=1).then_inc(c, 1)
                for gr in range(2):
                    v = selu[:, gr, :].rearrange("p (h d) -> p h d", h=H)
                    g.affine_select(out=v, in_=v, compare_op=ALU.not_equal, fill=1.0, base=128 * gr,
                                    pattern=[[-32, H], [-1, DH]], channel_multiplier=1).then_inc(c, 1)
                v = selb[:, :].rearrange("p (h d) -> p h d", h=H)
                g.affine_select(out=v, in_=v, compare_op=ALU.not_equal, fill=1.0, base=0,
                                pattern=[[-1, H], [0, DH]], channel_multiplier=1).then_inc(c, 1)
                g.affine_select(out=ltri[:, :], in_=ltri[:, :], compare_op=ALU.is_gt, fill=0.0, base=0,
                                pattern=[[1, P]], channel_multiplier=-1).then_inc(c, 1)
                g.memset(onesb[:, :], 1.0).then_inc(c, 1)
                g.memset(vt[:, :, :, :, DH:DH + 1], 1.0).then_inc(c, 1)
                g.memset(nm[:, :, :], 0.0).then_inc(c, 1)
                g.iota(tio_i[:, :], pattern=[[1, T + 1]], base=0, channel_multiplier=0).then_inc(S["numbered"], 1)
                hold(c, N_CONST)

            def high_low(steps, dst_hi, dst_lo, src, tmp=None, moving=False):
                if moving:
                    steps.step(g.tensor_tensor(dst_hi, src, zero[:, :].to_broadcast(src.shape), ALU.add))
                else:
                    steps.step(g.tensor_scalar(dst_hi, src, 1.0, 0.0, ALU.mult, ALU.add))
                steps.step(g.tensor_tensor(tmp if tmp is not None else dst_lo, src, dst_hi, ALU.subtract))

            def split_chunk(n, n_pair, par):
                steps = Steps(hold, S["chunk_steps"], n, 2)
                hold(w_in[par], n_pair * 16 + 16)
                col = n * CH
                high_low(steps, W[:, bass.ds(col, CH)], W[:, bass.ds(col + WLEN, CH)], stage[:, par, :], moving=True)
                steps.end()

            def slot(b):
                pbt = b.plus(2)
                if pbt.within(0, B - 1):
                    st = Steps(hold, S["prep_steps"], pbt.n, ENGINE_STEPS["prep"])
                    hold(S["st1_ready"], b.n + 3)
                    if pbt.within(0, 0):
                        hold(S["sb_ready"], 1)
                    if pbt.within(2, B - 1):
                        hold(S["queries_out"], b.n * 48 + 48)
                    mean, var = mv1[:, pbt.parity, 0:1], mv1[:, pbt.parity, 1:2]
                    st.step(g.tensor_scalar(psc[:, 0:1], var, EPS, 1.0, ALU.add, ALU.mult))
                    st.step(g.tensor_tensor(psc[:, 1:2], psc[:, 0:1], mhalf[:, :], ALU.pow))
                    st.step(g.tensor_tensor(psc[:, 2:3], psc[:, 1:2], sb_col[:, bass.ds(pbt.n, 1)], ALU.mult))
                    st.step(g.tensor_scalar(psc[:, 3:4], mean, -1.0, 0.0, ALU.mult, ALU.add))
                    st.step(g.tensor_tensor(norm[:, :], xres[:, bass.ds(pbt.n, 1), :].rearrange("p o q -> p (o q)"),
                                            psc[:, 3:4].to_broadcast([P, L]), ALU.add))
                    st.step(g.tensor_scalar(norm[:, :], norm[:, :], psc[:, 2:3], 0.0, ALU.mult, ALU.add))
                    pt = parts[:, pbt.parity]
                    high_low(st, pt[:, 0, :], None, norm[:, :], rest[:, :])
                    high_low(st, pt[:, 1, :], pt[:, 2, :], rest[:, :])
                    st.end()
                    g.nop().then_inc(S["prep_done"], 1)
                    if b.within(-2, -2):
                        constants()
                if b.within(1, 1):
                    for n in range(2):
                        pool.dma_start(stage[:, n, :], wpack[0, :, n * CH:(n + 1) * CH]).then_inc(w_in[n], 16)
                if b.within(2, 1 + NCH):
                    n = b.n - 2
                    split_chunk(n, b.pair - 1, b.parity)
                    if b.within(2, NCH - 1):
                        pool.dma_start(stage[:, b.parity, :], wpack[0, :, bass.ds((n + 2) * CH, CH)]) \
                            .then_inc(w_in[b.parity], 16)
                    if b.within(1 + NCH, 1 + NCH):
                        g.nop().then_inc(S["w_ready"], 1)
                pv2 = b.plus(-2)
                if pv2.within(0, B - 1):
                    hold(S["idx_ready"], b.n - 1)
                    for a in range(2):
                        pool.indirect_dma_start(
                            out=zs[:, :], out_offset=bass.IndirectOffsetOnAxis(ap=idx[:, b.parity, a:a + 1], axis=0),
                            in_=z[:, b.parity, :], in_offset=None).then_inc(slots_out[b.parity], 16)
                lb = b.plus(3)
                if lb.within(1, 1):
                    hold(S["first_keys"], 1)
                if lb.within(1, B - 1):
                    st = Steps(hold, S["keys_steps"], lb.n, ENGINE_STEPS["keys"])
                    hold(loads[lb.parity], lb.pair * 32 + 32)
                    if lb.within(2, B - 1):
                        hold(S["keys_out"], b.n * 48 + 96)
                    pt = parts[:, lb.parity]
                    high_low(st, pt[:, 3, :], None, cin[:, lb.parity, :], rest[:, :])
                    high_low(st, pt[:, 4, :], pt[:, 5, :], rest[:, :])
                    st.end()
                pv = b.plus(-1)
                if pv.within(0, B - 1):
                    hold(S["t_ready"], b.n)
                    if pv.within(1, B - 1):
                        hold(S["x1_kept"], b.n - 1)
                    xr = xres[:, bass.ds(pv.n, 1), :].rearrange("p o q -> p (o q)")
                    g.tensor_tensor(x1[:, :], xr, tb[:, :], ALU.add).then_inc(S["x1_ready"], 1)
                    hold(S["st2_ready"], b.n)
                    st = Steps(hold, S["z_steps"], pv.n, ENGINE_STEPS["z"])
                    if pv.within(2, B - 1):
                        hold(S["zt_ps"], b.n - 2)
                        hold(slots_out[pv.parity], pv.pair * 32)
                    st.step(g.tensor_scalar(zsc[:, 0:1], mv2[:, 1:2], EPS, 1.0, ALU.add, ALU.mult))
                    st.step(g.tensor_tensor(zsc[:, 1:2], zsc[:, 0:1], mhalf[:, :], ALU.pow))
                    st.step(g.tensor_scalar(zsc[:, 2:3], mv2[:, 0:1], -1.0, 0.0, ALU.mult, ALU.add))
                    st.step(g.tensor_scalar(z[:, pv.parity, :], x1[:, :], zsc[:, 2:3], zsc[:, 1:2], ALU.add, ALU.mult))
                    st.end()
                    g.nop().then_inc(S["z_ready"], 1)

            slots(pool, slot)

            def expert(e, e_par):
                def load(ch):
                    pool.dma_start(stage2[:, ch % 2, :], wpack[bass.ds(e, 1), :, ch * CH2:(ch + 1) * CH2].rearrange(
                        "o p c -> p (o c)")).then_inc(w2_in[ch % 2], 16)

                for ch in range(2):
                    load(ch)
                for ch in range(NCH2):
                    steps = Steps(hold, S["chunk2_steps"], (e - 1) * NCH2 + ch, 2)
                    hold(w2_in[ch % 2], (e - 1) * (8 * NCH2) + (16 * (ch // 2) + 16))
                    col = e_par * half + ch * CH2
                    high_low(steps, W[:, col:col + CH2], W[:, col + WLEN:col + WLEN + CH2], stage2[:, ch % 2, :])
                    steps.end()
                    if ch + 2 < NCH2:
                        load(ch + 2)
                g.nop().then_inc(S["w_ready"], 1)

            hold(S["attn_done"], 1)
            hold(S["tables_done"], 1)
            hold(xrow_in[0], 16)
            expert(1, 1)
            with pool.Fori(1, E // 2) as i:
                for par in range(2):
                    e = i * 2 + par
                    last = pool.value_load(etab[0:1, 1, bass.ds(e - 2, 1)], min_val=1, max_val=T + 1)
                    hold(S["tiles_done"], last)
                    expert(e, par)

            hold(y_out[0], 16 * ((T + 1) // 2))
            hold(y_out[1], 16 * (T // 2))

            def gather(b, r):
                for a in range(2):
                    pool.indirect_dma_start(
                        out=gb[:, r, a, :], out_offset=None, in_=ys[:, :],
                        in_offset=bass.IndirectOffsetOnAxis(ap=fidx[:, b, a:a + 1], axis=0)) \
                        .then_inc(g_in[r], 16)

            for b in range(B):
                if b >= 4:
                    hold(S["comb_done"], b - 3)
                gather(b, b % 4)

        @block.scalar
        def _(act):
            s = nc.scalar
            act.wait_ge(S["len_in"], 16)
            s.activation(len_f[:, :], len_i[:, :], ACT.Copy).then_inc(S["ln_ready"], 1)
            act.wait_ge(S["ln_ready"], 1)
            s.activation(sb_col[:, :], len_f[:, :], ACT.Ln).then_inc(S["ln_ready"], 1)

            def slot(b):
                nb, pv, pv2 = b.plus(1), b.plus(-1), b.plus(-2)
                full, behind = b.within(0, B - 1), pv.within(0, B - 1)

                if b.within(-2, -2):
                    act.wait_ge(S["rows_set"], 3)
                    s.activation(ks[MROW:MROW + 2], ks[MROW:MROW + 2], ACT.Copy, bias=1.0).then_inc(S["rows_set"], 1)

                def exps(w, us_):
                    if not full:
                        return
                    for u in us_:
                        j, kk = u // 2, u % 2
                        if u == 0 and (w >= 2 or b.within(1, B - 1)):
                            act.wait_ge(S["pv_done"], b.n * 4 + (w - 1))
                        act.wait_ge(S["scores_ready"], b.n * 32 + (8 * w + u + 1))
                        s.activation(probs[:, w % 2, j, kk, :], sc[u % 2][:, :], ACT.Exp) \
                            .then_inc(S["exp_done"], 1)

                def take_out(bb, gr):
                    act.wait_ge(S["pv_done"], bb.n * 4 + 2 * gr + 2)
                    if bb.within(1, B - 1):
                        act.wait_ge(S["u_ready"], bb.n)
                        act.wait_ge(S["sums_out"], bb.n * 32)
                    s.activation(og[:, gr, :], ob[:, :], ACT.Copy).then_inc(S["og_ready"], 1)

                exps(0, range(0, 3))
                if pv2.within(0, B - 1):
                    act.wait_ge(S["zt_ps"], b.n - 1)
                    if b.within(3, B + 1):
                        act.wait_ge(S["gate_ready"], b.n - 2)
                    s.activation(zt[:, :, :].rearrange("p k t -> p (k t)"), misc[:, :], ACT.Copy) \
                        .then_inc(S["zt_ready"], 1)
                exps(0, range(3, 6))
                if pv.within(0, B - 1):
                    take_out(pv, 1)
                exps(0, range(6, 8))
                if nb.within(0, B - 1):
                    act.wait_ge(S["vt_ps"], b.n + 2)
                    s.activation(vt[:, nb.parity, :, :, 0:DH], misc[:, :].rearrange("p (k h d) -> p k h d", k=4, h=H),
                                 ACT.Copy).then_inc(S["vt_ready"], 1)
                exps(1, range(0, 4))
                if pv.within(0, B - 1):
                    act.wait_ge(S["u_ready"], b.n)
                    if pv.within(1, B - 1):
                        act.wait_ge(S["t_ready"], b.n - 1)
                    s.activation(us[:, :], misc[:, :], ACT.Copy).then_inc(S["us_ready"], 1)
                exps(1, range(4, 8))
                exps(2, range(6))
                if full:
                    take_out(b, 0)
                exps(2, range(6, 8))
                exps(3, range(0, 5))
                if behind:
                    act.wait_ge(S["x1_ready"], b.n)
                    s.activation(xres[:, bass.ds(pv.n, 1), :].rearrange("p o q -> p (o q)"), x1[:, :], ACT.Copy) \
                        .then_inc(S["x1_kept"], 1)
                exps(3, range(5, 8))

            slots(act, slot)

            act.wait_ge(S["routed"], 1)
            s.activation(gexp[:, :], gexp[:, :], ACT.Exp).then_inc(S["gexp_ready"], 1)

            act.wait_ge(S["cv_zero"], 1)
            act.wait_ge(S["zero_ready"], 1)
            for e in range(1, E, 2):
                r = act.value_load(etab[0:1, 0, e:e + 1], min_val=0, max_val=E * REG - P)
                act.dma_start(zs[bass.ds(r, P), :], cv[:, :]).then_inc(S["zero_out"], 16)
            s.activation(len_f[:, 0:1], zero[:, :], ACT.Silu).then_inc(S["table_prep"], 1)

            def x_high(t, par):
                act.wait_ge(S["xt_ps"], t + 1)
                s.activation(xT[:, par, 0], misc[:, :].rearrange("p (k t) -> p k t", k=KD), ACT.Copy) \
                    .then_inc(S["xt_hi"], 1)

            def tile(t, par, first=False, last=False):
                if not first:
                    act.wait_ge(S["h_ready"], t * 2)
                for n in range(2):
                    act.wait_ge(S["up_ready"], t * 2 + n + 1)
                    s.activation(act_g[:, n * 512:(n + 1) * 512], up[n][0], ACT.Silu).then_inc(S["silu_done"], 1)
                if not last:
                    x_high(t + 1, 1 - par)
                act.wait_ge(S["ht_ps"], t + 1)
                for n in range(2):
                    s.activation(hT[:, par, 0, 4 * n:4 * n + 4, :], hTp[n][:, :].rearrange("p (k t) -> p k t", k=4),
                                 ACT.Copy).then_inc(S["ht_hi"], 1)

            x_high(0, 0)
            tile(0, 0, first=True)
            with act.Fori(0, (T - 3) // 2) as i:
                tile(i * 2 + 1, 1)
                tile(i * 2 + 2, 0)
            tile(T - 2, 1)
            tile(T - 1, 0, last=True)

        @block.vector
        def _(dve):
            v = nc.vector
            dve.wait_ge(S["ln_ready"], 2)
            v.tensor_scalar(sb_col[:, :], sb_col[:, :], SCALE, None, ALU.mult).then_inc(S["sb_ready"], 1)
            def number():
                dve.wait_ge(S["consts"], N_CONST)

                st = Steps(dve.wait_ge, S["table_chain"], 0, 5)
                dve.wait_ge(S["numbered"], 1)
                st.step(v.tensor_copy(tio[:, 0, :], tio_i[:, :]))
                st.step(v.tensor_copy(numbers[:, :], tio_i[:, 0:E]))
                st.step(v.tensor_scalar(first_rows[:, :], numbers[:, :], float(REG), None, ALU.mult))
                st.step(v.tensor_scalar(tio[:, 1, :], tio[:, 0, :], float(P), None, ALU.mult))
                st.step(v.tensor_tensor(upto[:, :, :], numbers[:, :].unsqueeze(2).to_broadcast([P, E, E]),
                                        numbers[:, :].unsqueeze(1).to_broadcast([P, E, E]), ALU.is_ge))
                st.end()

            def set_rows():
                v.memset(mask_sum[:, :], 0.0).then_inc(S["rows_set"], 1)
                v.memset(ks[96:128], 0.0).then_inc(S["rows_set"], 1)
                v.memset(qs[96:128], 0.0).then_inc(S["rows_set"], 1)
                dve.wait_ge(S["rows_set"], 3)

            def slot(b):
                nb, pv, pv2, ahead2 = b.plus(1), b.plus(-1), b.plus(-2), b.plus(2)

                def maxima(ks_):
                    for i in ks_:
                        k = (i + LEAD) % 16
                        bb = nb if i + LEAD < 16 else ahead2
                        if not bb.within(0, B - 1):
                            continue
                        if k == 0 and bb.within(2, B - 1):
                            dve.wait_ge(S["mt_ready"], bb.n - 1)
                        dve.wait_ge(S["p1_ready"], bb.n * 16 + (k + 1))
                        v.tensor_reduce(nm[:, bb.parity, 2 * k:2 * k + 2],
                                        p1[k % 2][:, :].rearrange("p (c k) -> p c k", c=2), AX_X, ALU.max,
                                        negate=True).then_inc(S["p1_used"], 1)

                routes = pv2.within(0, B - 1)
                maxima(range(0, 2))
                if routes:
                    a_steps = Steps(dve.wait_ge, S["route_a_steps"], pv2.n, ENGINE_STEPS["route_a"])
                    dve.wait_ge(S["gate_ready"], b.n - 1)
                    two = experts2[:, bass.ds(pv2.n, 1), :].rearrange("p o a -> p (o a)")
                    v.nop().then_inc(S["dve_held"], 1)
                    a_steps.step(v.max(sorted8[:, :], misc[:, 0:E]))
                    v.nop().then_inc(S["dve_held"], 1)
                    a_steps.step(v.max_index(order8[:, :], sorted8[:, :], misc[:, 0:E]))
                    v.nop().then_inc(S["gate_used"], 1)
                maxima(range(2, 3))
                if routes:
                    a_steps.step(v.tensor_copy(scores2[:, bass.ds(pv2.n, 1), :].rearrange("p o a -> p (o a)"),
                                               sorted8[:, 0:2]))
                    a_steps.step(v.tensor_copy(two, order8[:, 0:2]))
                    a_steps.step(v.tensor_tensor(masks[:, :, :], numbers[:, :].unsqueeze(1).to_broadcast([P, 2, E]),
                                                 two.unsqueeze(2).to_broadcast([P, 2, E]), ALU.is_equal))
                    a_steps.step(v.tensor_tensor(maskb[:, :], masks[:, 0, :], masks[:, 1, :], ALU.add))
                    a_steps.end()
                    v.nop().then_inc(S["mask_ready"], 1)
                maxima(range(3, 6))
                lb = b.plus(3)
                if lb.within(0, B - 1):
                    dve.wait_ge(loads[lb.parity], lb.pair * 32 + 32)
                    if lb.within(2, B - 1):
                        dve.wait_ge(S["prep_done"], b.n + 2)
                    if lb.within(1, B - 1):
                        dve.wait_ge(S["st1_ready"], b.n + 3)
                    v.bn_stats(st1[:, :], xres[:, bass.ds(lb.n, 1), :].rearrange("p o q -> p (o q)")) \
                        .then_inc(S["st1_steps"], 1)
                    dve.wait_ge(S["st1_steps"], b.n + 4)
                    v.nop().then_inc(S["dve_held"], 1)
                    v.bn_aggr(mv1[:, lb.parity, :], st1[:, :]).then_inc(S["st1_ready"], 1)
                maxima(range(6, 7))
                if pv.within(0, B - 1):
                    dve.wait_ge(S["den_in"], b.n * 16)
                    if pv.within(1, B - 1):
                        dve.wait_ge(S["rec_out"], b.n * 16 - 16)
                    v.reciprocal(rden[:, :], den[:, :]).then_inc(S["rec_ready"], 1)
                maxima(range(7, 8))
                if routes:
                    b_steps = Steps(dve.wait_ge, S["route_b_steps"], pv2.n, ENGINE_STEPS["route_b"])
                    dve.wait_ge(S["rank_ready"], b.n - 1)
                    b_steps.step(v.tensor_tensor(place[:, 2, :], misc[:, 0:E], first_rows[:, :], ALU.add))
                    v.nop().then_inc(S["rank_used"], 1)
                    b_steps.step(v.tensor_tensor(mask_sum[:, :], mask_sum[:, :], maskb[:, :], ALU.add))
                    b_steps.step(v.tensor_tensor(place[:, 0:2, :], masks[:, :, :],
                                                 place[:, 2, :].unsqueeze(1).to_broadcast([P, 2, E]), ALU.mult))
                maxima(range(8, 9))
                if routes:
                    row = rows[:, bass.ds(pv2.n, 1), :].rearrange("p o a -> p (o a)")
                    b_steps.step(v.tensor_reduce(row, place[:, 0:2, :], AX_X, ALU.add))
                    if b.within(4, B + 1):
                        dve.wait_ge(slots_out[pv2.parity], pv2.pair * 32)
                    v.nop().then_inc(S["dve_held"], 1)
                    b_steps.step(v.tensor_copy(idx[:, b.parity, :], row))
                    b_steps.end()
                    v.nop().then_inc(S["idx_ready"], 1)
                maxima(range(9, 10))
                if b.within(-3, -3):
                    k_steps = Steps(dve.wait_ge, S["keys_steps"], 0, ENGINE_STEPS["keys"])
                    pt = parts[:, 0]
                    k_steps.step(v.tensor_copy(pt[:, 3, :], cin[:, 0, :]))
                    k_steps.step(v.tensor_tensor(us[:, :], cin[:, 0, :], pt[:, 3, :], ALU.subtract))
                    k_steps.step(v.tensor_copy(pt[:, 4, :], us[:, :]))
                    k_steps.step(v.tensor_tensor(pt[:, 5, :], us[:, :], pt[:, 4, :], ALU.subtract))
                    k_steps.end()
                    v.nop().then_inc(S["first_keys"], 1)
                if b.within(-2, -2):
                    set_rows()
                maxima(range(10, 12))
                if nb.within(0, B - 1):
                    dve.wait_ge(S["mt_ready"], b.n + 2)
                    if nb.within(1, B - 1):
                        dve.wait_ge(S["m_out"], b.n * 16 + 16)
                    v.tensor_copy(mrow[:, 0, :], misc[0:32, 0:P]).then_inc(S["m_steps"], 1)
                    dve.wait_ge(S["m_steps"], b.n + 2)
                    v.tensor_tensor(mrow[:, 1, :], misc[0:32, 0:P], mrow[:, 0, :], ALU.subtract) \
                        .then_inc(S["m_ready"], 1)
                maxima(range(12, 13))
                if pv.within(0, B - 1):
                    dve.wait_ge(S["r_ready"], b.n)
                    dve.wait_ge(S["us_ready"], b.n)
                    if pv.within(1, B - 1):
                        dve.wait_ge(S["x1_ready"], b.n - 1)
                    v.tensor_tensor(tb[:, :], misc[:, :], us[:, :], ALU.mult).then_inc(S["t_ready"], 1)
                maxima(range(13, 15))
                if b.within(-2, -2):
                    number()
                if pv.within(0, B - 1):
                    dve.wait_ge(S["x1_ready"], b.n)
                    if pv.within(1, B - 1):
                        dve.wait_ge(S["st2_ready"], b.n - 1)
                    v.bn_stats(st2[:, :], x1[:, :]) \
                        .then_inc(S["st2_steps"], 1)
                    dve.wait_ge(S["st2_steps"], b.n)
                    if pv.within(1, B - 1):
                        dve.wait_ge(S["z_ready"], b.n - 1)
                    v.nop().then_inc(S["dve_held"], 1)
                    v.bn_aggr(mv2[:, :], st2[:, :]).then_inc(S["st2_ready"], 1)
                maxima(range(15, 16))
                if b.within(B, B):
                    v.memset(cv[:, :], 0.0).then_inc(S["cv_zero"], 1)

            slots(dve, slot)

            st = Steps(dve.wait_ge, S["table_chain"], 1, 5)
            link = st.step
            dve.wait_ge(S["pv_done"], 4 * B)
            link(v.tensor_tensor(gexp[:, :].unsqueeze(2), scores2[:, :, 1:2], scores2[:, :, 0:1], ALU.subtract))
            v.nop().then_inc(S["routed"], 1)
            chosen = experts2[:, :, :].rearrange("p b a -> p (b a)").unsqueeze(2)
            link(v.tensor_tensor(c3, numbers[:, :].unsqueeze(1).to_broadcast([P, 2 * B, E]),
                                 chosen.to_broadcast([P, 2 * B, E]), ALU.is_equal))
            dve.wait_ge(S["cnt_ready"], 1)
            cnt = misc[:, 0:E]
            link(v.tensor_tensor(zero_rows, cnt, first_rows[:, :], ALU.add))
            link(v.tensor_copy(etab[:, 0, :], zero_rows))
            v.nop().then_inc(S["zero_ready"], 1)
            link(v.tensor_tensor(k3, cnt.unsqueeze(2).to_broadcast([P, E, B]),
                                 tio[:, 1, 0:B].unsqueeze(1).to_broadcast([P, E, B]), ALU.is_gt))
            link(v.tensor_reduce(tiles, k3, AX_X, ALU.add))
            link(v.tensor_tensor(upto[:, :, :], upto[:, :, :], tiles.unsqueeze(1).to_broadcast([P, E, E]), ALU.mult))
            link(v.tensor_reduce(cum, upto[:, :, :], AX_X, ALU.add))
            link(v.tensor_scalar(etab[:, 1, :], cum, 1.0, None, ALU.add))
            link(v.tensor_tensor(t3, tio[:, 0, 0:T].unsqueeze(2).to_broadcast([P, T, E - 1]),
                                 cum[:, 0:E - 1].unsqueeze(1).to_broadcast([P, T, E - 1]), ALU.is_ge))
            link(v.tensor_reduce(expt, t3, AX_X, ALU.add))
            link(v.tensor_scalar(tab[:, 2, 0:T], expt, 1.0, None, ALU.add))
            link(v.tensor_copy(tab[:, 1, 0:T], expt))
            link(v.tensor_scalar(tab[:, 1, 0:T], tab[:, 1, 0:T], 1, None, ALU.bitwise_and))
            link(v.tensor_scalar(delta, tiles, -float(P), float(REG), ALU.mult, ALU.add))
            link(v.tensor_tensor(t3, t3, delta[:, 0:E - 1].unsqueeze(1).to_broadcast([P, T, E - 1]), ALU.mult))
            link(v.tensor_reduce(row_t, t3, AX_X, ALU.add))
            link(v.tensor_tensor(row_t, row_t, tio[:, 1, 0:T], ALU.add))
            link(v.tensor_scalar(tab[:, 0, 0:T], row_t, zero_rows[:, E - 1:E], None, ALU.min))
            link(v.tensor_scalar(tab[:, 3, :], tio[:, 0, :], cum[:, E - 1:E], None, ALU.is_le))
            v.nop().then_inc(S["tab_ready"], 1)
            link(v.tensor_tensor(tbase, cum, tiles, ALU.subtract))
            link(v.scalar_tensor_tensor(base, tbase, -float(P), first_rows[:, :], ALU.mult, ALU.add))
            link(v.tensor_tensor(c3, c3, base.unsqueeze(1).to_broadcast([P, 2 * B, E]), ALU.mult))
            link(v.tensor_reduce(at_base, c3, AX_X, ALU.add))
            link(v.tensor_tensor(fidx[:, :, :], rows[:, :, :],
                                 at_base.rearrange("p (b a) -> p b a", a=2), ALU.subtract))
            v.nop().then_inc(S["tables_done"], 1)
            dve.wait_ge(S["gexp_ready"], 1)
            link(v.tensor_scalar(gate[:, 1, :], gexp[:, :], 1.0, None, ALU.add))
            link(v.reciprocal(gate[:, 0, :], gate[:, 1, :]))
            link(v.tensor_tensor(gate[:, 1, :], gexp[:, :], gate[:, 0, :], ALU.mult))

            def x_low(t, par):
                dve.wait_ge(S["xt_hi"], t + 1)
                v.tensor_tensor(xT[:, par, 1], misc[:, :].rearrange("p (k t) -> p k t", k=KD), xT[:, par, 0],
                                ALU.subtract).then_inc(S["xt_lo"], 1)

            def take_y(t, par, early=False):
                dve.wait_ge(S["tiles_done"], t + 2)
                if not early:
                    dve.wait_ge(y_out[par], (t - par) * 8)
                v.tensor_copy(yb[:, par, :], ob[:, :]).then_inc(S["yb_ready"], 1)

            def tile(t, par, first=False, last=False, early=False):
                if not first:
                    dve.wait_ge(S["ht_ps"], t)
                for n in range(2):
                    dve.wait_ge(S["silu_done"], t * 2 + n + 1)
                    v.tensor_tensor(hbuf[:, n * 512:(n + 1) * 512], up[n][1], act_g[:, n * 512:(n + 1) * 512],
                                    ALU.mult).then_inc(S["h_ready"], 1)
                if not last:
                    x_low(t + 1, 1 - par)
                if not first:
                    take_y(t - 1, 1 - par, early)
                for n in range(2):
                    dve.wait_ge(S["ht_hi"], t * 2 + n + 1)
                    v.tensor_tensor(hT[:, par, 1, 4 * n:4 * n + 4, :], hTp[n][:, :].rearrange("p (k t) -> p k t", k=4),
                                    hT[:, par, 0, 4 * n:4 * n + 4, :], ALU.subtract).then_inc(S["ht_lo"], 1)

            x_low(0, 0)
            tile(0, 0, first=True)
            tile(1, 1, early=True)
            tile(2, 0, early=True)
            with dve.Fori(1, (T - 3) // 2) as i:
                tile(i * 2 + 1, 1)
                tile(i * 2 + 2, 0)
            tile(T - 2, 1)
            tile(T - 1, 0, last=True)
            take_y(T - 1, 0)

            v.nop().then_inc(S["comb_steps"], 1)
            with dve.Fori(0, B // 4) as i:
                for r in range(4):
                    b = i * 4 + r
                    dve.wait_ge(g_in[r], i * 32 + 32)
                    xr = xres[:, bass.ds(b, 1), :].rearrange("p o q -> p (o q)")
                    v.scalar_tensor_tensor(xr, gb[:, r, 0, :], gate[:, 0, bass.ds(b, 1)], xr, ALU.mult, ALU.add) \
                        .then_inc(S["comb_steps"], 1)
                    dve.wait_ge(S["comb_steps"], b + 2)
                    v.scalar_tensor_tensor(xr, gb[:, r, 1, :], gate[:, 1, bass.ds(b, 1)], xr, ALU.mult, ALU.add) \
                        .then_inc(S["comb_done"], 1)

        @block.tensor
        def _(pe):
            m = nc.tensor
            pe.wait_ge(S["consts"], N_CONST)
            pe.wait_ge(S["gate_in"], 16)

            def slot(b):
                nb, pv, pv2 = b.plus(1), b.plus(-1), b.plus(-2)
                full, ahead = b.within(0, B - 1), nb.within(0, B - 1)
                behind = pv.within(0, B - 1)
                def rows_unit(i):
                    k = (i + LEAD) % 16
                    bb = nb if i + LEAD < 16 else b.plus(2)
                    if not bb.within(0, B - 1):
                        return
                    hh, qh = k // 2, k % 2
                    if k % 8 == 0:
                        pe.wait_ge(st_in[bb.parity][k // 8], bb.pair * 32 + 32)
                    if k >= 2 or bb.within(1, B - 1):
                        pe.wait_ge(S["p1_used"], bb.n * 16 + (k - 1))
                    for c in range(2):
                        q0 = (2 * qh + c) * P
                        ins = m.matmul(p1[k % 2][:, c * 512:(c + 1) * 512], qs[0:KROWS, bb.parity, hh, q0:q0 + P],
                                       ks[0:KROWS, bb.parity, hh, :], start=True, stop=True)
                    ins.then_inc(S["p1_ready"], 1)

                def score(w, u):
                    j, kk = u // 2, u % 2
                    h, kc = 4 * (w // 2) + j, 2 * (w % 2) + kk
                    if w == 0 and u == 0:
                        if b.within(0, 0):
                            pe.wait_ge(S["rows_set"], 4)
                        pe.wait_ge(S["m_in"], b.n * 16 + 16)
                    if w or u >= 2 or b.within(1, B - 1):
                        pe.wait_ge(S["exp_done"], b.n * 32 + (8 * w + u - 1))
                    m.matmul(sc[u % 2][:, :], ks[:, b.parity, h, kc * P:(kc + 1) * P], qs[:, b.parity, h, :],
                             start=True, stop=True).then_inc(S["scores_ready"], 1)

                def values(bb, w, kk):
                    pe.wait_ge(S["exp_done"], bb.n * 32 + (8 * w + 7 + kk))
                    if kk == 0:
                        if w == 0:
                            pe.wait_ge(S["vt_ready"], bb.n + 1)
                        if w == 2 or (w == 0 and bb.within(1, B - 1)):
                            pe.wait_ge(S["og_ready"], bb.n * 2 + w // 2)
                    kc = 2 * (w % 2) + kk
                    for j in range(4):
                        ins = m.matmul(ob[32 * j:32 * j + 32, :], vt[:, bb.parity, kc, 4 * (w // 2) + j, :],
                                       probs[:, w % 2, j, kk, :], start=(kc == 0), stop=(kc == 3))
                    if kk == 1:
                        ins.then_inc(S["pv_done"], 1)

                reader = (S["t_ready"], b.n - 1) if pv2.within(0, B - 1) else \
                    (S["m_ready"], b.n + 1) if full else None

                for w in range(4):
                    for u in range(8):
                        if u % 2 == 0:
                            rows_unit(4 * w + u // 2)
                        if full:
                            score(w, u)
                        if (w, u) == (0, 2) and pv2.within(0, B - 1):
                            pe.wait_ge(S["z_ready"], b.n - 1)
                            pe.wait_ge(*reader)
                            for k in range(KD):
                                ins = m.transpose(misc[:, k * P:(k + 1) * P], z[:, b.parity, k * P:(k + 1) * P],
                                                  ident[:, :])
                            ins.then_inc(S["zt_ps"], 1)
                            reader = (S["zt_ready"], b.n - 1)
                        if (w, u) == (0, 4) and pv2.within(0, B - 1):
                            pe.wait_ge(*reader)
                            for k in range(KD):
                                ins = m.matmul(misc[:, 0:E], zt[:, k, :], gw[:, k, :], start=(k == 0),
                                               stop=(k == KD - 1))
                            ins.then_inc(S["gate_ready"], 1)
                            reader = (S["gate_used"], b.n - 1)
                        if u in (1, 5):
                            kk = u // 4
                            if w == 0 and behind:
                                values(pv, 3, kk)
                            if w > 0 and full:
                                values(b, w - 1, kk)
                        if (w, u) == (0, 7) and ahead:
                            pe.wait_ge(S["cv_in"], b.n * 16 + 32)
                            if reader:
                                pe.wait_ge(*reader)
                            for kc in range(4):
                                ins = m.transpose(misc[:, kc * P:(kc + 1) * P], cv[:, kc * P:(kc + 1) * P], ident[:, :])
                            ins.then_inc(S["vt_ps"], 1)
                            reader = (S["vt_ready"], b.n + 2)
                        if (w, u) == (1, 2) and behind:
                            if reader:
                                pe.wait_ge(*reader)
                            pe.wait_ge(S["og_ready"], b.n * 2)
                            for gr in range(2):
                                ins = m.matmul(misc[:, :], selu[:, gr, :], og[:, gr, :], start=(gr == 0),
                                               stop=(gr == 1))
                            ins.then_inc(S["u_ready"], 1)
                            reader = (S["us_ready"], b.n)
                        if (w, u) == (1, 6) and pv2.within(0, B - 1):
                            pe.wait_ge(*reader)
                            pe.wait_ge(S["mask_ready"], b.n - 1)
                            m.matmul(misc[:, 0:E], ltri[:, :], maskb[:, :], start=True, stop=False)
                            m.matmul(misc[:, 0:E], onesb[:, :], mask_sum[:, :], start=False, stop=True) \
                                .then_inc(S["rank_ready"], 1)
                            reader = (S["rank_used"], b.n - 1)
                        if (w, u) == (3, 0) and ahead:
                            pe.wait_ge(S["p1_used"], b.n * 16 + 32)
                            if reader:
                                pe.wait_ge(*reader)
                            m.transpose(misc[:, 0:P], nm[:, nb.parity, :], ident[:, :]).then_inc(S["mt_ready"], 1)
                            reader = (S["m_ready"], b.n + 2)
                        if (w, u) == (3, 1) and behind:
                            pe.wait_ge(S["rec_in"], b.n * 16)
                            if reader:
                                pe.wait_ge(*reader)
                            m.matmul(misc[:, :], selb[:, :], r8[:, :], start=True, stop=True).then_inc(S["r_ready"], 1)
                            reader = (S["t_ready"], b.n)

            slots(pe, slot)
            pe.wait_ge(S["og_ready"], 2 * B)
            m.nop().then_inc(S["attn_done"], 1)
            pe.wait_ge(S["rank_used"], B)
            pe.wait_ge(S["route_b_steps"], ENGINE_STEPS["route_b"] * B)
            m.matmul(misc[:, 0:E], onesb[:, :], mask_sum[:, :], start=True, stop=True).then_inc(S["cnt_ready"], 1)

            pe.wait_ge(S["tab_ready"], 1)
            m.nop().then_inc(S["tiles_done"], 1)

            def x_tile(t, par, first=False):
                pe.wait_ge(xrow_in[par], (t - par) * 8 + 16)
                if not first:
                    pe.wait_ge(S["xt_lo"], t)
                for k in range(KD):
                    ins = m.transpose(misc[:, k * P:(k + 1) * P], xrow[:, par, k * P:(k + 1) * P], ident[:, :])
                ins.then_inc(S["xt_ps"], 1)

            def split_products(bank, stat, w_off, n_chunks, stride, col):
                for k in range(n_chunks):
                    for n, (s_part, w_part) in enumerate(((0, 0), (0, 1), (1, 0))):
                        at_w = w_off + (w_part * WLEN + col + k * stride)
                        ins = m.matmul(bank, stat[:, s_part, k, :], W[:, bass.ds(at_w, 512)],
                                       start=(k == 0 and n == 0), stop=(k == n_chunks - 1 and n == 2))
                return ins

            def half_of(t):
                e = pe.value_load(tab[0:1, 1, bass.ds(t, 1)], min_val=0, max_val=1)
                return e * half

            def up_tile(t, par, first=False):
                ready = pe.value_load(tab[0:1, 2, bass.ds(t, 1)], min_val=1, max_val=E)
                off = half_of(t)
                pe.wait_ge(S["w_ready"], ready)
                pe.wait_ge(S["xt_lo"], t + 1)
                for n in range(2):
                    if not first:
                        pe.wait_ge(S["h_ready"], t * 2 - 1 + n)
                    for wn in range(2):
                        ins = split_products(up[n][wn], xT[:, par], off, KD, I, wn * KD * I + n * 512)
                    ins.then_inc(S["up_ready"], 1)

            def down_tile(t, par, first=False):
                off = half_of(t)
                pe.wait_ge(S["ht_lo"], t * 2 + 2)
                if not first:
                    pe.wait_ge(S["yb_ready"], t)
                ins = split_products(ob[:, :], hT[:, par], off, KI, D, 2 * KD * I)
                ins.then_inc(S["tiles_done"], 1)

            def h_tile(t, par, first=False):
                pe.wait_ge(S["h_ready"], t * 2 + 2)
                if not first:
                    pe.wait_ge(S["ht_lo"], t * 2)
                for k in range(KI):
                    ins = m.transpose(hTp[k // 4][:, (k % 4) * P:(k % 4 + 1) * P], hbuf[:, k * P:(k + 1) * P],
                                      ident[:, :])
                ins.then_inc(S["ht_ps"], 1)

            def tile(t, par, last=False, second=False):
                up_tile(t, par)
                if not last:
                    x_tile(t + 1, 1 - par)
                down_tile(t - 1, 1 - par, first=second)
                h_tile(t, par)

            def maybe_tile(t, par, last=False):
                before_needed = pe.value_load(tab[0:1, 3, bass.ds(t, 1)], min_val=0, max_val=1)
                needed = pe.value_load(tab[0:1, 3, bass.ds(t + 1, 1)], min_val=0, max_val=1)
                with pe.If(needed > 0):
                    tile(t, par, last)
                with pe.Else():
                    pe.wait_ge(S["xt_lo"], t + 1)
                    pe.wait_ge(S["h_ready"], t * 2)
                    for n in range(2):
                        m.nop().then_inc(S["up_ready"], 1)
                    if not last:
                        pe.wait_ge(xrow_in[1 - par], (t + 1 - (1 - par)) * 8 + 16)
                        m.nop().then_inc(S["xt_ps"], 1)
                    with pe.If(before_needed > 0):
                        down_tile(t - 1, 1 - par)
                    with pe.Else():
                        pe.wait_ge(S["ht_lo"], t * 2)
                        pe.wait_ge(S["yb_ready"], t - 1)
                        m.nop().then_inc(S["tiles_done"], 1)
                    pe.wait_ge(S["h_ready"], t * 2 + 2)
                    m.nop().then_inc(S["ht_ps"], 1)

            x_tile(0, 0, first=True)
            up_tile(0, 0, first=True)
            x_tile(1, 1)
            h_tile(0, 0, first=True)
            tile(1, 1, second=True)
            tile(2, 0)
            with pe.Fori(1, SURE // 2) as i:
                tile(i * 2 + 1, 1)
                tile(i * 2 + 2, 0)
            with pe.Fori(SURE // 2, (T - 3) // 2) as i:
                maybe_tile(i * 2 + 1, 1)
                maybe_tile(i * 2 + 2, 0)
            maybe_tile(T - 2, 1)
            maybe_tile(T - 1, 0, last=True)
            needed = pe.value_load(tab[0:1, 3, T:T + 1], min_val=0, max_val=1)
            with pe.If(needed > 0):
                down_tile(T - 1, 0)
            with pe.Else():
                pe.wait_ge(S["ht_lo"], 2 * T)
                pe.wait_ge(S["yb_ready"], T - 1)
                m.nop().then_inc(S["tiles_done"], 1)


def kernel(x, ctx_2048, itok_B_779_1933, L0_ffn_gate_w, L0_ffn_w1, L0_ffn_w2, L0_ffn_w3):
    import concourse.bacc as _bacc
    from concourse.bass_utils import run_bass_kernel_spmd as _run

    def chunked(w):
        w = np.asarray(w)
        e, o, i = w.shape
        return w.transpose(0, 2, 1).reshape(e, i // P, P, o).transpose(0, 2, 1, 3).reshape(e, P, i // P * o)

    arrays = {
        "x_dram": np.ascontiguousarray(x),
        "ctx_dram": np.ascontiguousarray(ctx_2048),
        "lengths_dram": np.ascontiguousarray(itok_B_779_1933),
        "wpack_dram": np.ascontiguousarray(np.concatenate(
            [chunked(L0_ffn_w1), chunked(L0_ffn_w3), chunked(L0_ffn_w2)], axis=2)),
        "gate_dram": np.ascontiguousarray(np.asarray(L0_ffn_gate_w).T),
    }
    nc = _bacc.Bacc("TRN2", target_bir_lowering=False, num_devices=1)
    args = [nc.dram_tensor(n, a.shape, mybir.dt.from_np(a.dtype), kind="ExternalInput").ap() for n, a in arrays.items()]
    out = nc.dram_tensor("out_dram", arrays["x_dram"].shape, F32, kind="ExternalOutput").ap()
    build(nc, *args, out)
    r = _run(nc, [arrays], core_ids=[0])
    return r.results[0]["out_dram"]
```
